# Optimizing a Trainium2 kernel written in Bass

```python
import numpy as np
import jax
import jax.numpy as jnp

def _softmax(x, axis=-1):
    return jax.nn.softmax(x, axis=axis)

def _gelu(x):
    return jax.nn.gelu(x, approximate=True)

def _silu(x):
    return jax.nn.silu(x)

def _sigmoid(x):
    return jax.nn.sigmoid(x)

def _layernorm(x, axis=-1, eps=1e-05):
    m = jnp.mean(x, axis=axis, keepdims=True)
    v = jnp.var(x, axis=axis, keepdims=True)
    return (x - m) / jnp.sqrt(v + eps)

def _scatter_add(tgt, idx, src, axis=0):
    return tgt.at[idx].add(src)

def _segment_sum(src, seg, n):
    return jax.ops.segment_sum(src, seg, n)
kernel_name = 'mk_sandwich_d2_jaxref_r4_1eff1b'

def setup_inputs(seed: int=0):
    np.random.seed(seed)
    _w = jnp.asarray

    def _L0_attn_setup():
        import math
        import jax, jax.numpy as jnp
        import numpy as np
        H = 16
        LAYER_POS = 12
        LAM_INIT = 0.8 - 0.6 * math.exp(-0.3 * (LAYER_POS - 1))
        LN_EPS = 1e-05

        def _heads(t, B, S, h, d):
            return t.reshape(B, S, h, d).transpose(0, 2, 1, 3)
        key = jax.random.key(seed)
        ks = jax.random.split(key, 12)
        B, S, E = (2, 512, 256)
        d = E // H
        w = 0.02
        return {'x': jax.random.normal(ks[0], (B, S, E), jnp.float32), 'Wq1': jax.random.normal(ks[1], (E, E), jnp.float32) * w, 'Wq2': jax.random.normal(ks[2], (E, E), jnp.float32) * w, 'Wk1': jax.random.normal(ks[3], (E, E), jnp.float32) * w, 'Wk2': jax.random.normal(ks[4], (E, E), jnp.float32) * w, 'Wv': jax.random.normal(ks[5], (E, 2 * E), jnp.float32) * w, 'Wo': jax.random.normal(ks[6], (2 * E, E), jnp.float32) * w, 'lq1': jax.random.normal(ks[7], (H, d), jnp.float32) * 0.1, 'lk1': jax.random.normal(ks[8], (H, d), jnp.float32) * 0.1, 'lq2': jax.random.normal(ks[9], (H, d), jnp.float32) * 0.1, 'lk2': jax.random.normal(ks[10], (H, d), jnp.float32) * 0.1}
    _L0_attn_in = _L0_attn_setup()

    def _L0_ffn_setup():
        import jax, jax.numpy as jnp
        import numpy as np
        EMB = 256
        FF = 4 * EMB

        def _ternary(w):
            scale = jnp.maximum(jnp.mean(jnp.abs(w)), 1e-08)
            w_t = jnp.clip(jnp.round(w / scale), -1.0, 1.0)
            return w + jax.lax.stop_gradient(w_t - w)
        key = jax.random.key(seed)
        kx, k1, k2, kb1, kb2 = jax.random.split(key, 5)
        x = jax.random.normal(kx, (4, 512, EMB), dtype=jnp.float32)
        lim1 = 1.0 / np.sqrt(EMB)
        lim2 = 1.0 / np.sqrt(FF)
        W1 = jax.random.uniform(k1, (FF, EMB), jnp.float32, -lim1, lim1)
        b1 = jax.random.uniform(kb1, (FF,), jnp.float32, -lim1, lim1)
        W2 = jax.random.uniform(k2, (EMB, FF), jnp.float32, -lim2, lim2)
        b2 = jax.random.uniform(kb2, (EMB,), jnp.float32, -lim2, lim2)
        return {'x': x, 'W1': W1, 'b1': b1, 'W2': W2, 'b2': b2}
    _L0_ffn_in = _L0_ffn_setup()

    def _L1_attn_setup():
        import jax, jax.numpy as jnp
        import numpy as np
        from jax import lax
        B, T, D = (8, 1024, 256)
        H, K = (16, 15)

        def _forward(inputs, W1, b1, W2, b2, conv_shared_weight):
            h = jnp.einsum('btd,de->bte', inputs, W1) + b1
            a, g = jnp.split(h, 2, axis=-1)
            x = a * jax.nn.sigmoid(g)
            w = jax.nn.softmax(conv_shared_weight, axis=-1)
            r = D // H
            filt = jnp.repeat(w.T.reshape(-1), r).reshape(K, D)
            filt = filt[:, None, :]
            conv = lax.conv_general_dilated(x, filt, window_strides=(1,), padding='SAME', dimension_numbers=('NHC', 'HIO', 'NHC'), feature_group_count=D)
            return jnp.einsum('btd,de->bte', conv, W2) + b2
        key = jax.random.key(seed)
        k0, k1, k2, k3 = jax.random.split(key, 4)
        scale1 = 1.0 / np.sqrt(D)
        return {'inputs': jax.random.normal(k0, (B, T, D), dtype=jnp.float32), 'W1': jax.random.normal(k1, (D, 2 * D), dtype=jnp.float32) * scale1, 'b1': jnp.zeros((2 * D,), dtype=jnp.float32), 'W2': jax.random.normal(k2, (D, D), dtype=jnp.float32) * scale1, 'b2': jnp.zeros((D,), dtype=jnp.float32), 'conv_shared_weight': jax.random.normal(k3, (H, K), dtype=jnp.float32)}
    _L1_attn_in = _L1_attn_setup()

    def _L1_ffn_setup():
        import jax, jax.numpy as jnp
        import numpy as np
        DIM = 256
        E = 16
        TOPK = 2
        G = 4
        TOPK_G = 2
        INTER = 128
        N_SHARED = 2
        ROUTE_SCALE = 1.0

        def _gate(xf, gate_w, gate_b):
            scores = xf @ gate_w.T
            scores = jax.nn.softmax(scores.astype(jnp.float32), axis=-1)
            orig = scores
            scores = scores + gate_b
            T = xf.shape[0]
            sg = scores.reshape(T, G, E // G)
            group_scores = jax.lax.top_k(sg, 2)[0].sum(-1)
            _, gidx = jax.lax.top_k(group_scores, TOPK_G)
            keep = jax.nn.one_hot(gidx, G).sum(axis=1) > 0
            sg = jnp.where(keep[:, :, None], sg, -jnp.inf)
            scores = sg.reshape(T, E)
            _, idx = jax.lax.top_k(scores, TOPK)
            weights = jnp.take_along_axis(orig, idx, axis=1)
            weights = (weights * ROUTE_SCALE).astype(xf.dtype)
            return (weights, idx)
        key = jax.random.key(seed)
        ks = jax.random.split(key, 16)
        s = lambda fan_in: 1.0 / np.sqrt(fan_in)
        inp = {'x': jax.random.normal(ks[0], (4, 256, DIM), dtype=jnp.float32), 'gate_w': jax.random.normal(ks[1], (E, DIM), dtype=jnp.float32) * s(DIM), 'gate_b': jnp.zeros((E,), dtype=jnp.float32), 'We1': jax.random.normal(ks[2], (E, DIM, INTER), dtype=jnp.float32) * s(DIM), 'be1': jnp.zeros((E, INTER), dtype=jnp.float32), 'We2': jax.random.normal(ks[3], (E, INTER, DIM), dtype=jnp.float32) * s(INTER), 'be2': jnp.zeros((E, DIM), dtype=jnp.float32), 'We3': jax.random.normal(ks[4], (E, DIM, INTER), dtype=jnp.float32) * s(DIM), 'be3': jnp.zeros((E, INTER), dtype=jnp.float32), 'ws1': jax.random.normal(ks[5], (DIM, N_SHARED * INTER), dtype=jnp.float32) * s(DIM), 'bs1': jnp.zeros((N_SHARED * INTER,), dtype=jnp.float32), 'ws2': jax.random.normal(ks[6], (N_SHARED * INTER, DIM), dtype=jnp.float32) * s(N_SHARED * INTER), 'bs2': jnp.zeros((DIM,), dtype=jnp.float32), 'ws3': jax.random.normal(ks[7], (DIM, N_SHARED * INTER), dtype=jnp.float32) * s(DIM), 'bs3': jnp.zeros((N_SHARED * INTER,), dtype=jnp.float32)}
        return inp
    _L1_ffn_in = _L1_ffn_setup()
    _d = {'L0_attn_x': _L0_attn_in['x'], 'L0_attn_Wq1': _L0_attn_in['Wq1'], 'L0_attn_Wq2': _L0_attn_in['Wq2'], 'L0_attn_Wk1': _L0_attn_in['Wk1'], 'L0_attn_Wk2': _L0_attn_in['Wk2'], 'L0_attn_Wv': _L0_attn_in['Wv'], 'L0_attn_Wo': _L0_attn_in['Wo'], 'L0_attn_lq1': _L0_attn_in['lq1'], 'L0_attn_lk1': _L0_attn_in['lk1'], 'L0_attn_lq2': _L0_attn_in['lq2'], 'L0_attn_lk2': _L0_attn_in['lk2'], 'L0_ffn_W1': _L0_ffn_in['W1'], 'L0_ffn_b1': _L0_ffn_in['b1'], 'L0_ffn_W2': _L0_ffn_in['W2'], 'L0_ffn_b2': _L0_ffn_in['b2'], 'L1_attn_W1': _L1_attn_in['W1'], 'L1_attn_b1': _L1_attn_in['b1'], 'L1_attn_W2': _L1_attn_in['W2'], 'L1_attn_b2': _L1_attn_in['b2'], 'L1_attn_conv_shared_weight': _L1_attn_in['conv_shared_weight'], 'L1_ffn_gate_w': _L1_ffn_in['gate_w'], 'L1_ffn_gate_b': _L1_ffn_in['gate_b'], 'L1_ffn_We1': _L1_ffn_in['We1'], 'L1_ffn_be1': _L1_ffn_in['be1'], 'L1_ffn_We2': _L1_ffn_in['We2'], 'L1_ffn_be2': _L1_ffn_in['be2'], 'L1_ffn_We3': _L1_ffn_in['We3'], 'L1_ffn_be3': _L1_ffn_in['be3'], 'L1_ffn_ws1': _L1_ffn_in['ws1'], 'L1_ffn_bs1': _L1_ffn_in['bs1'], 'L1_ffn_ws2': _L1_ffn_in['ws2'], 'L1_ffn_bs2': _L1_ffn_in['bs2'], 'L1_ffn_ws3': _L1_ffn_in['ws3'], 'L1_ffn_bs3': _L1_ffn_in['bs3']}
    _x0 = _d['L0_attn_x']
    _d['L0_attn_x'] = jax.random.normal(jax.random.fold_in(jax.random.key(seed), 1), (8, 1024, 256), dtype=_x0.dtype)
    del _x0
    return _d

def reference(L0_attn_x, L0_attn_Wq1, L0_attn_Wq2, L0_attn_Wk1, L0_attn_Wk2, L0_attn_Wv, L0_attn_Wo, L0_attn_lq1, L0_attn_lk1, L0_attn_lq2, L0_attn_lk2, L0_ffn_W1, L0_ffn_b1, L0_ffn_W2, L0_ffn_b2, L1_attn_W1, L1_attn_b1, L1_attn_W2, L1_attn_b2, L1_attn_conv_shared_weight, L1_ffn_gate_w, L1_ffn_gate_b, L1_ffn_We1, L1_ffn_be1, L1_ffn_We2, L1_ffn_be2, L1_ffn_We3, L1_ffn_be3, L1_ffn_ws1, L1_ffn_bs1, L1_ffn_ws2, L1_ffn_bs2, L1_ffn_ws3, L1_ffn_bs3):

    def _L0_attn_ref(x, Wq1, Wq2, Wk1, Wk2, Wv, Wo, lq1, lk1, lq2, lk2):
        import math
        import jax, jax.numpy as jnp
        import numpy as np
        H = 16
        LAYER_POS = 12
        LAM_INIT = 0.8 - 0.6 * math.exp(-0.3 * (LAYER_POS - 1))
        LN_EPS = 1e-05

        def _heads(t, B, S, h, d):
            return t.reshape(B, S, h, d).transpose(0, 2, 1, 3)
        B, S, E = x.shape
        d = E // H
        scale = 1.0 / math.sqrt(d)
        q1 = _heads(x @ Wq1, B, S, H, d)
        q2 = _heads(x @ Wq2, B, S, H, d)
        k1 = _heads(x @ Wk1, B, S, H, d)
        k2 = _heads(x @ Wk2, B, S, H, d)
        v = _heads(x @ Wv, B, S, H, 2 * d)
        causal = jnp.tril(jnp.ones((S, S), dtype=bool))
        neg_inf = jnp.float32(-jnp.inf)
        s1 = jnp.einsum('bhqd,bhkd->bhqk', q1, k1) * scale
        s2 = jnp.einsum('bhqd,bhkd->bhqk', q2, k2) * scale
        a1 = jax.nn.softmax(jnp.where(causal, s1, neg_inf), axis=-1)
        a2 = jax.nn.softmax(jnp.where(causal, s2, neg_inf), axis=-1)
        lam = jnp.exp(jnp.sum(lq1 * lk1, axis=-1)) - jnp.exp(jnp.sum(lq2 * lk2, axis=-1)) + LAM_INIT
        comb = a1 - lam[None, :, None, None] * a2
        out = jnp.einsum('bhqk,bhkv->bhqv', comb, v)
        mu = jnp.mean(out, axis=-1, keepdims=True)
        var = jnp.mean(jnp.square(out - mu), axis=-1, keepdims=True)
        normed = (out - mu) * jax.lax.rsqrt(var + LN_EPS)
        scaled = normed * (1.0 - LAM_INIT)
        merged = scaled.transpose(0, 2, 1, 3).reshape(B, S, 2 * E)
        return merged @ Wo

    def _L0_ffn_ref(x, W1, b1, W2, b2):
        import jax, jax.numpy as jnp
        import numpy as np
        EMB = 256
        FF = 4 * EMB

        def _ternary(w):
            scale = jnp.maximum(jnp.mean(jnp.abs(w)), 1e-08)
            w_t = jnp.clip(jnp.round(w / scale), -1.0, 1.0)
            return w + jax.lax.stop_gradient(w_t - w)
        h = jnp.einsum('bsd,fd->bsf', x, _ternary(W1)) + b1
        h = jax.nn.gelu(h, approximate=False)
        out = jnp.einsum('bsf,df->bsd', h, _ternary(W2)) + b2
        return out

    def _L1_attn_ref(inputs, W1, b1, W2, b2, conv_shared_weight):
        import jax, jax.numpy as jnp
        import numpy as np
        from jax import lax
        B, T, D = (8, 1024, 256)
        H, K = (16, 15)

        def _forward(inputs, W1, b1, W2, b2, conv_shared_weight):
            h = jnp.einsum('btd,de->bte', inputs, W1) + b1
            a, g = jnp.split(h, 2, axis=-1)
            x = a * jax.nn.sigmoid(g)
            w = jax.nn.softmax(conv_shared_weight, axis=-1)
            r = D // H
            filt = jnp.repeat(w.T.reshape(-1), r).reshape(K, D)
            filt = filt[:, None, :]
            conv = lax.conv_general_dilated(x, filt, window_strides=(1,), padding='SAME', dimension_numbers=('NHC', 'HIO', 'NHC'), feature_group_count=D)
            return jnp.einsum('btd,de->bte', conv, W2) + b2
        return _forward(inputs, W1, b1, W2, b2, conv_shared_weight)

    def _L1_ffn_ref(x, gate_w, gate_b, We1, be1, We2, be2, We3, be3, ws1, bs1, ws2, bs2, ws3, bs3):
        import jax, jax.numpy as jnp
        import numpy as np
        DIM = 256
        E = 16
        TOPK = 2
        G = 4
        TOPK_G = 2
        INTER = 128
        N_SHARED = 2
        ROUTE_SCALE = 1.0

        def _gate(xf, gate_w, gate_b):
            scores = xf @ gate_w.T
            scores = jax.nn.softmax(scores.astype(jnp.float32), axis=-1)
            orig = scores
            scores = scores + gate_b
            T = xf.shape[0]
            sg = scores.reshape(T, G, E // G)
            group_scores = jax.lax.top_k(sg, 2)[0].sum(-1)
            _, gidx = jax.lax.top_k(group_scores, TOPK_G)
            keep = jax.nn.one_hot(gidx, G).sum(axis=1) > 0
            sg = jnp.where(keep[:, :, None], sg, -jnp.inf)
            scores = sg.reshape(T, E)
            _, idx = jax.lax.top_k(scores, TOPK)
            weights = jnp.take_along_axis(orig, idx, axis=1)
            weights = (weights * ROUTE_SCALE).astype(xf.dtype)
            return (weights, idx)
        shape = x.shape
        xf = x.reshape(-1, DIM)
        weights, idx = _gate(xf, gate_w, gate_b)
        combine = (jax.nn.one_hot(idx, E, dtype=xf.dtype) * weights[..., None]).sum(1)
        h1 = jnp.einsum('td,edi->tei', xf, We1) + be1
        h3 = jnp.einsum('td,edi->tei', xf, We3) + be3
        h = jax.nn.silu(h1) * h3
        yo = jnp.einsum('tei,eid->ted', h, We2) + be2
        y = jnp.einsum('te,ted->td', combine, yo)
        z = jax.nn.silu(xf @ ws1 + bs1) * (xf @ ws3 + bs3) @ ws2 + bs2
        return (y + z).reshape(shape)
    x = L0_attn_x
    x = x + _layernorm(_L0_attn_ref(_layernorm(x, axis=-1), L0_attn_Wq1, L0_attn_Wq2, L0_attn_Wk1, L0_attn_Wk2, L0_attn_Wv, L0_attn_Wo, L0_attn_lq1, L0_attn_lk1, L0_attn_lq2, L0_attn_lk2), axis=-1)
    x = x + _layernorm(_L0_ffn_ref(_layernorm(x, axis=-1), L0_ffn_W1, L0_ffn_b1, L0_ffn_W2, L0_ffn_b2), axis=-1)
    x = x + _layernorm(_L1_attn_ref(_layernorm(x, axis=-1), L1_attn_W1, L1_attn_b1, L1_attn_W2, L1_attn_b2, L1_attn_conv_shared_weight), axis=-1)
    x = x + _layernorm(_L1_ffn_ref(_layernorm(x, axis=-1), L1_ffn_gate_w, L1_ffn_gate_b, L1_ffn_We1, L1_ffn_be1, L1_ffn_We2, L1_ffn_be2, L1_ffn_We3, L1_ffn_be3, L1_ffn_ws1, L1_ffn_bs1, L1_ffn_ws2, L1_ffn_bs2, L1_ffn_ws3, L1_ffn_bs3), axis=-1)
    return x

_drawn_inputs = setup_inputs


def setup_inputs(seed=0):
    import zlib

    import numpy as np

    out = dict(_drawn_inputs(seed))
    spreads = {'L1_attn_b1': (0.0, 0.1),
     'L1_attn_b2': (0.0, 0.1),
     'L1_ffn_gate_b': (0.0, 0.1),
     'L1_ffn_be1': (0.0, 0.648),
     'L1_ffn_be2': (0.0, 0.39),
     'L1_ffn_be3': (0.0, 0.676),
     'L1_ffn_bs1': (0.0, 0.1),
     'L1_ffn_bs2': (0.0, 0.1),
     'L1_ffn_bs3': (0.0, 0.1)}
    factors = {'L0_ffn_b1': 24.651, 'L0_ffn_b2': 64.0}
    for name, (base, spread) in spreads.items():
        noise = np.random.default_rng([zlib.crc32(name.encode()), seed]).standard_normal(out[name].shape)
        drawn = base * np.exp(spread * noise) if base else spread * noise
        out[name] = jnp.asarray(drawn.astype(out[name].dtype))
    for name, factor in factors.items():
        out[name] = (out[name] * factor).astype(out[name].dtype)
    return out
```

```python
import math
from contextlib import ExitStack

import concourse.bass as bass
from concourse import mybir

F32, BF16 = mybir.dt.float32, mybir.dt.bfloat16
ALU, ACT, AX = mybir.AluOpType, mybir.ActivationFunctionType, mybir.AxisListType

P = 128
B, S, E = 8, 1024, 256
H, D = 16, 16
VD = 2 * D
VC = VD + 1
EC = E // P
GT = 4
GN = GT * P
G = B * S // GN
GB = S // GN
SB = S // P
MATS = 4
FF = 4 * E
FM = FF // P
K = 15
PAD = K // 2
NE, NG, INTER, NSH = 16, 4, 128, 2
NX = NE + NSH
EPG = NE // NG
EPS = 1e-5
LAM_INIT = 0.8 - 0.6 * math.exp(-0.3 * (12 - 1))
MASKED = -1e30
BIG = 1e30


class Chain:

    def __init__(self, eng, sem, per_turn=0):
        self.eng, self.sem, self.per, self.base, self.n = eng, sem, per_turn, 0, 0

    def turn(self, g):
        assert self.n in (0, self.per), (self.n, self.per)
        self.base, self.n = g * self.per, 0

    def mark(self, ins):
        ins.then_inc(self.sem, 1)
        self.n += 1

    def wait(self):
        self.eng.wait_ge(self.sem, self.base + self.n)

    def link(self, ins):
        self.mark(ins)
        self.wait()


def at(ap, g):
    one = ap[g:g + 1] if isinstance(g, int) else ap[bass.ds(g, 1)]
    names = [f"d{n}" for n in range(len(ap.shape) - 1)]
    return one.rearrange(f"a {' '.join(names)} -> (a {names[0]}) {' '.join(names[1:])}")


def turns(eng, n, unroll, body):
    for r in range(unroll):
        body(r, 0, r, unroll)
    with eng.Fori(1, n // unroll - 1) as i:
        for r in range(unroll):
            body(i * unroll + r, i, r, unroll)
    i = n // unroll - 1
    for r in range(unroll):
        body(i * unroll + r, i, r, unroll - 1 - r)


def wait_pos(eng, sem, value):
    if not isinstance(value, int) or value > 0:
        eng.wait_ge(sem, value)


def wait_apart(eng, go, sem, value):
    if isinstance(value, int):
        eng.wait_ge(sem, value)
        return
    with eng.register() as count:
        eng.reg_mov(count, value)
        eng.wait_ge(go, 1)
        eng.wait_ge(sem, count)


class Mem:

    def __init__(self, nc, ctx, tag):
        self.nc, self.ctx, self.tag = nc, ctx, tag

    def sb(self, name, shape, dt=F32):
        return self.ctx.enter_context(self.nc.sbuf_tensor(f"{self.tag}_{name}", shape, dt))

    def ps(self, name, shape=(P, 512)):
        return self.ctx.enter_context(self.nc.psum_tensor(f"{self.tag}_{name}", list(shape), F32))

    def sem(self, name):
        return self.nc.semaphore(f"{self.tag}_{name}").__enter__()

    def sems(self, name, n):
        return [self.sem(f"{name}{i}") for i in range(n)]


def mean_var(v, chain, go, src, stats, mv, tiles):
    for t in range(tiles):
        chain.mark(v.bn_stats(stats[:, t, :], src(t)))
    wait_apart(v, go, chain.sem, chain.base + chain.n)
    for t in range(tiles):
        chain.mark(v.bn_aggr(mv[:, t, :], stats[:, t, :]))
    chain.wait()


def bcast(ap, shape):
    return ap.to_broadcast(shape)


def prepare(nc, m, I, C):
    with ExitStack() as ctx:
        t = Mem(nc, ctx, "pre")
        wload, small = t.sem("wload"), t.sem("small")
        zeroed, poolc, vec, acts, tot = (t.sem(n) for n in ("zeroed", "poolc", "vec", "acts", "tot"))
        ones = t.sb("ones", [P, P])
        absw = t.sb("absw", [P, FF * EC])
        part = t.sb("part", [P, 2])
        thr = t.sb("thr", [P, 2, 2])
        neg = t.sb("neg", [P, FF * EC])
        lqk = t.sb("lqk", [P, 4, H * D])
        lsum = t.sb("lsum", [P, 2, H])
        fmax = t.sb("fmax", [P, EC])
        fsum = t.sb("fsum", [P, EC])
        psum = t.ps("tot")
        block = ctx.enter_context(nc.Block())

        @block.sync
        def _(sp):
            sp.dma_start(C["wqk"][:], I["wqk"].rearrange("m (c p) n -> p m c n", p=P)).then_inc(C["s_qkv"], 16)
            sp.dma_start(C["wv"][:], I["Wv"].rearrange("(c p) n -> p c n", p=P)).then_inc(C["s_qkv"], 16)
            sp.dma_start(C["w1t"][:], I["w1t"].rearrange("(c p) n -> p c n", p=P)).then_inc(wload, 16)
            sp.dma_start(C["w2t"][:], I["w2t"].rearrange("(c p) n -> p c n", p=P)).then_inc(wload, 16)
            for h in range(H):
                r = h * D % P
                sp.dma_start(C["filt"][r:r + D, h * D // P, :],
                             I["cw"][h, :].partition_broadcast(D)).then_inc(small, 16)
            for n, name in enumerate(("lq1", "lk1", "lq2", "lk2")):
                sp.dma_start(lqk[:, n, :], I[name].rearrange("h d -> (h d)").partition_broadcast(P)).then_inc(small, 16)
            n0 = 0
            for name in ("xw1", "xw3"):
                we, ws = {"xw1": ("We1", "ws1"), "xw3": ("We3", "ws3")}[name]
                for c in range(EC):
                    sp.dma_start(C[name][:, c, 0:NE], I[we].rearrange("e (c p) n -> c p e n", p=P)[c]).then_inc(C["s_moe"], 16)
                    sp.dma_start(C[name][:, c, NE:NX], I[ws].rearrange("(c p) (x n) -> c p x n", p=P, x=NSH)[c]).then_inc(C["s_moe"], 16)
                    n0 += 2
            sp.dma_start(C["xw2"][:, 0:NE], I["We2"].rearrange("e p n -> p e n")).then_inc(C["s_moe"], 16)
            sp.dma_start(C["xw2"][:, NE:NX], I["ws2"].rearrange("(x p) n -> p x n", p=P)).then_inc(C["s_moe"], 16)
            sp.dma_start(C["xb1"][:], I["xb1"]).then_inc(C["s_moe"], 16)
            sp.dma_start(C["xb3"][:], I["xb3"]).then_inc(C["s_moe"], 16)
            sp.dma_start(C["xb2"][:], I["be2"]).then_inc(C["s_moe"], 16)
            sp.dma_start(C["bs2"][:], I["bs2"].partition_broadcast(P)).then_inc(C["s_moe"], 16)
            sp.dma_start(C["gw"][:], I["gw"].rearrange("(c p) e -> p c e", p=P)).then_inc(C["s_moe"], 16)
            n0 += 7
            for t in range(GT):
                sp.dma_start(C["gb"][:, t], I["gb"].partition_broadcast(P)).then_inc(C["s_moe"], 16)
                n0 += 1
            C["n_moe"] = 16 * n0
            sp.dma_start(C["wo"][:], I["Wo"].rearrange("(c p) n -> p c n", p=P)).then_inc(C["s_ffn"], 16)
            sp.dma_start(C["b1"][:], I["b1"]).then_inc(C["s_ffn"], 16)
            sp.dma_start(C["b2"][:], I["b2"].partition_broadcast(P)).then_inc(C["s_ffn"], 16)
            sp.dma_start(C["cw1"][:], I["cw1"].rearrange("(c p) n -> p c n", p=P)).then_inc(C["s_conv"], 16)
            sp.dma_start(C["cw2"][:], I["cw2"].rearrange("(c p) n -> p c n", p=P)).then_inc(C["s_conv"], 16)
            sp.dma_start(C["cb1"][:], I["cb1"]).then_inc(C["s_conv"], 16)
            sp.dma_start(C["cb2"][:], I["cb2"].partition_broadcast(P)).then_inc(C["s_conv"], 16)

        @block.gpsimd
        def _(pool):
            pool.memset(C["ident"][:], 0.0).then_inc(zeroed, 1)
            pool.memset(C["mask"][:], 0.0).then_inc(zeroed, 1)
            pool.memset(C["identb"][:], 0.0).then_inc(zeroed, 1)
            pool.memset(C["tri_g"][:], 1.0).then_inc(zeroed, 1)
            pool.memset(C["tri_e"][:], 1.0).then_inc(zeroed, 1)
            pool.memset(C["neghalf"][:], -0.5).then_inc(zeroed, 1)
            pool.wait_ge(zeroed, 6)
            for x in ("ident", "identb"):
                pool.affine_select(out=C[x][:], in_=C[x][:], compare_op=ALU.not_equal, fill=1.0, base=0,
                                   pattern=[[-1, P]], channel_multiplier=1).then_inc(poolc, 1)
            pool.affine_select(out=C["mask"][:], in_=C["mask"][:], compare_op=ALU.is_ge, fill=MASKED, base=0,
                               pattern=[[-1, P]], channel_multiplier=1).then_inc(poolc, 1)
            pool.affine_select(out=C["tri_g"][:], in_=C["tri_g"][:], compare_op=ALU.is_gt, fill=0.0, base=0,
                               pattern=[[1, NG], [-1, NG]], channel_multiplier=0).then_inc(poolc, 1)
            pool.affine_select(out=C["tri_e"][:], in_=C["tri_e"][:], compare_op=ALU.is_gt, fill=0.0, base=0,
                               pattern=[[1, NE], [-1, NE]], channel_multiplier=0).then_inc(poolc, 1)
            pool.wait_ge(poolc, 5)

        @block.tensor
        def _(pe):
            pe.wait_ge(vec, 3)
            nc.tensor.matmul(psum[:, 0:2], ones[:], part[:], start=True, stop=True).then_inc(tot, 1)

        @block.scalar
        def _(act):
            act.wait_ge(vec, 9)
            nc.scalar.activation(lsum[:], lsum[:], ACT.Exp).then_inc(acts, 1)
            for c in range(EC):
                nc.scalar.activation(C["filt"][:, c, :], C["filt"][:, c, :], ACT.Exp).then_inc(acts, 1)

        @block.vector
        def _(v):
            ch = Chain(v, vec)
            v.sem_inc(C["go"], 1)
            ch.mark(v.memset(ones[:], 1.0))
            v.wait_ge(wload, 32)
            w = [C["w1t"][:].rearrange("p c n -> p (c n)"), C["w2t"][:].rearrange("p c n -> p (c n)")]
            for n in range(2):
                ch.mark(v.tensor_reduce(part[:, n:n + 1], w[n], AX.X, ALU.add, apply_absolute_value=True))
            assert ch.n == 3
            v.wait_ge(small, 16 * (H + 4))
            for n in range(2):
                ch.link(v.tensor_tensor(lqk[:, 2 * n, :], lqk[:, 2 * n, :], lqk[:, 2 * n + 1, :], ALU.mult))
                ch.mark(v.tensor_reduce(lsum[:, n, :], lqk[:, 2 * n, :].rearrange("p (h d) -> p h d", h=H), AX.X, ALU.add))
            ch.link(v.tensor_reduce(fmax[:], C["filt"][:], AX.X, ALU.max))
            assert ch.n == 8
            v.tensor_tensor(C["filt"][:], C["filt"][:], bcast(fmax[:].unsqueeze(2), [P, EC, K]), ALU.subtract).then_inc(vec, 1)
            ch.n += 1
            v.wait_ge(acts, 1 + EC)
            ch.link(v.tensor_tensor(lsum[:, 0, :], lsum[:, 1, :], lsum[:, 0, :], ALU.subtract))
            for b in range(B):
                ch.mark(v.tensor_scalar(C["neglam"][:, b * H:(b + 1) * H], lsum[:, 0, :], -LAM_INIT, None, ALU.add))
            ch.link(v.tensor_reduce(fsum[:], C["filt"][:], AX.X, ALU.add))
            ch.link(v.reciprocal(fsum[:], fsum[:]))
            ch.link(v.tensor_tensor(C["filt"][:], C["filt"][:], bcast(fsum[:].unsqueeze(2), [P, EC, K]), ALU.mult))
            v.wait_ge(tot, 1)
            ch.link(v.tensor_scalar(thr[:, :, 0], psum[:, 0:2], 1.0 / (FF * E), 1e-8, ALU.mult, ALU.max))
            ch.link(v.tensor_scalar(thr[:, :, 1], thr[:, :, 0], -0.5, None, ALU.mult))
            ch.link(v.tensor_scalar(thr[:, :, 0], thr[:, :, 0], 0.5, None, ALU.mult))
            for n in range(2):
                ch.mark(v.tensor_scalar(neg[:], w[n], thr[:, n, 1:2], None, ALU.is_lt))
                ch.link(v.tensor_scalar(absw[:], w[n], thr[:, n, 0:1], None, ALU.is_gt))
                ch.link(v.tensor_tensor(absw[:], absw[:], neg[:], ALU.subtract))
                ch.link(v.tensor_tensor(absw[:], absw[:], w[n], ALU.subtract))
                ch.link(v.tensor_tensor(w[n], w[n], absw[:], ALU.add))


def project(nc, I, C, x_in, parts, values):
    with ExitStack() as ctx:
        m = Mem(nc, ctx, "prj")
        x = m.sb("x", [P, 2, GT, E])
        xn = m.sb("xn", [P, GT, E])
        xt = m.sb("xt", [P, 2, EC, GN])
        stats, mv, var, rstd = m.sb("stats", [P, GT, 6]), m.sb("mv", [P, GT, 2]), m.sb("var", [P, GT]), m.sb("rstd", [P, GT])
        pt = m.sb("pt", [P, 4, 3, GN], BF16)
        rest = m.sb("rest", [P, 2, GN])
        vs = m.sb("vs", [P, 2, H, GT, VC])
        tp = [m.ps(f"tp{i}") for i in range(2)]
        qk = [m.ps(f"qk{i}") for i in range(4)]
        vp = [m.ps(f"v{i}") for i in range(2)]
        x_loaded, part_stored, v_stored = m.sems("x_loaded", 2), m.sems("part_stored", 4), m.sems("v_stored", 2)
        (stat, var_ready, rstd_ready, xn_ready, tp_ready, xt_ready, qk_ready, qk_split, hi_ready, split, parts_ready,
         v_ready, v_copied, ones_set) = (m.sem(n) for n in (
             "stat", "var_ready", "rstd_ready", "xn_ready", "tp_ready", "xt_ready", "qk_ready", "qk_split", "hi_ready",
             "split", "parts_ready", "v_ready", "v_copied", "ones_set"))
        NQ = MATS * EC
        xg = x_in.rearrange("(g t p) e -> g p t e", p=P, t=GT)
        pg = parts.rearrange("k m (b c p) (h n) -> b h m c p k n", b=B, c=EC, h=GB)
        vg = values.rearrange("(b h) p (c t v) -> b c p h (t v)", b=B, c=GB, t=GT)
        block = ctx.enter_context(nc.Block())

        @block.sync
        def _(sp):
            for g in range(2):
                sp.dma_start(x[:, g], at(xg, g)).then_inc(x_loaded[g], 16)

            def body(g, i, r, left):
                if left >= 2:
                    sp.wait_ge(xn_ready, g + 1)
                    sp.dma_start(x[:, r], at(xg, g + 2)).then_inc(x_loaded[r], 16)
                for n in range(NQ):
                    sp.wait_ge(parts_ready, g * NQ + n + 1)
                    sp.dma_start(part_dst(i, r, n), pt[:, n % 4]).then_inc(part_stored[n % 4], 16)
                sp.wait_ge(v_copied, g * GT + GT + 2)
                sp.dma_start(value_dst(i, r), vs[:, r].rearrange("p h t v -> p h (t v)")).then_inc(v_stored[r], 16)

            def part_dst(i, r, n):
                m0, c0 = n // EC, n % EC
                src = pg[:, r, m0, c0]
                return at(src, i)

            def value_dst(i, r):
                return at(vg[:, r], i)

            turns(sp, G, GB, body)
            for n in range(4):
                sp.wait_ge(part_stored[n], 16 * (G * NQ // 4 + 1))
            for r in range(2):
                sp.wait_ge(v_stored[r], 16 * (G // 2 + 1))

        @block.gpsimd
        def _(pool):
            pool.memset(vs[:, :, :, :, VD:VC].rearrange("p s h t o -> p (s h t) o"), 1.0).then_inc(ones_set, 1)

            def rstd_of(g):
                pool.wait_ge(var_ready, g + 1)
                nc.gpsimd.tensor_tensor(rstd[:], var[:], C["neghalf"][:, 0:GT], ALU.pow).then_inc(rstd_ready, 1)

            rstd_of(0)
            turns(pool, G, 2, lambda g, i, r, left: rstd_of(g + 1) if left else None)

        @block.vector
        def _(v):
            st = Chain(v, stat, 2 * GT)
            sp_ = Chain(v, split, NQ)
            v.sem_inc(qk_split, 4)

            def pre(g, r):
                st.turn(g)
                v.wait_ge(x_loaded[r], pre_load(g))
                mean_var(v, st, C["go"], lambda t: x[:, r, t], stats, mv, GT)
                v.tensor_scalar(var[:], mv[:, :, 1], EPS, None, ALU.add).then_inc(var_ready, 1)
                v.wait_ge(rstd_ready, g + 1)
                for t in range(GT):
                    ins = v.tensor_scalar(xn[:, t], x[:, r, t], mv[:, t, 0:1], rstd[:, t:t + 1], ALU.subtract, ALU.mult)
                ins.then_inc(xn_ready, 1)

            loads = {}

            def pre_load(g):
                return loads["n"]

            def body(g, i, r, left):
                sp_.turn(g)
                for n in range(NQ):
                    if n == 4 and left:
                        loads["n"] = 16 * (i + 1 + r)
                        pre(g + 1, (r + 1) % 2)
                    v.wait_ge(hi_ready, g * NQ + n + 1)
                    v.tensor_tensor(rest[:, n % 2], qk[n % 4][:], pt[:, n % 4, 0], ALU.subtract).then_inc(qk_split, 1)
                    v.wait_ge(qk_split, g * NQ + n + 1 + 4)
                    sp_.link(v.tensor_copy(pt[:, n % 4, 1], rest[:, n % 2]))
                    v.tensor_tensor(pt[:, n % 4, 2], rest[:, n % 2], pt[:, n % 4, 1], ALU.subtract).then_inc(parts_ready, 1)

            loads["n"] = 16
            pre(0, 0)
            turns(v, G, 2, body)

        @block.scalar
        def _(act):
            for n in range(4):
                act.sem_inc(part_stored[n], 16)
            for r in range(2):
                act.sem_inc(v_stored[r], 16)
            act.sem_inc(v_copied, 2)
            act.wait_ge(ones_set, 1)

            def xt_copy(g, r):
                for c in range(EC):
                    act.wait_ge(tp_ready, g * EC + c + 1)
                    act.activation(xt[:, r, c], tp[c][:], ACT.Copy).then_inc(xt_ready, 1)

            def body(g, i, r, left):
                for n in range(NQ):
                    act.wait_ge(qk_ready, g * NQ + n + 1)
                    act.wait_ge(part_stored[n % 4], 16 * (g * (NQ // 4) + n // 4 + 1))
                    act.activation(pt[:, n % 4, 0], qk[n % 4][:], ACT.Copy).then_inc(hi_ready, 1)
                if left:
                    xt_copy(g + 1, (r + 1) % 2)
                act.wait_ge(v_stored[r], 16 * (i + 1))
                for t in range(GT):
                    act.wait_ge(v_ready, g * GT + t + 1)
                    act.activation(vs[:, r, :, t, 0:VD], vp[t % 2][:].rearrange("p (h v) -> p h v", h=H),
                                   ACT.Copy).then_inc(v_copied, 1)

            xt_copy(0, 0)
            turns(act, G, 2, body)

        @block.tensor
        def _(pe):
            pe.wait_ge(C["s_qkv"], 32)

            def transposes(g):
                pe.wait_ge(xn_ready, g + 1)
                for c in range(EC):
                    for t in range(GT):
                        ins = nc.tensor.transpose(tp[c][:, t * P:(t + 1) * P], xn[:, t, c * P:(c + 1) * P], C["ident"][:])
                    ins.then_inc(tp_ready, 1)

            def body(g, i, r, left):
                pe.wait_ge(xt_ready, (g + 1) * EC)
                for n in range(NQ):
                    pe.wait_ge(qk_split, g * NQ + n + 1)
                    for c in range(EC):
                        ins = nc.tensor.matmul(qk[n % 4][:], C["wqk"][:, n // EC, c, n % EC * P:(n % EC + 1) * P],
                                               xt[:, r, c], start=(c == 0), stop=(c == EC - 1))
                    ins.then_inc(qk_ready, 1)
                if left:
                    transposes(g + 1)
                for t in range(GT):
                    pe.wait_ge(v_copied, g * GT + t + 1)
                    for c in range(EC):
                        ins = nc.tensor.matmul(vp[t % 2][:], xt[:, r, c, t * P:(t + 1) * P], C["wv"][:, c],
                                               start=(c == 0), stop=(c == EC - 1))
                    ins.then_inc(v_ready, 1)

            transposes(0)
            turns(pe, G, 2, body)


def attend(nc, I, C, parts, values, heads):
    PAIRS = [(0, 0), (0, 1), (1, 0), (1, 1), (0, 2), (2, 0)]
    KR = len(PAIRS) * D
    SL = 4
    T = B * H
    HB = GN // P
    SCALE = 1.0 / math.sqrt(D)
    MB = 64
    OW = MB + VC
    ST = [(half, j, mp, max(0, j - HB * half) * P) for half in (1, 0) for j in range(HB * (half + 1)) for mp in range(2)]
    NST = len(ST)
    at_st = {(half, j): n for n, (half, j, mp, off) in enumerate(ST) if mp}
    NSEL = 2 * 2 * HB
    ITEMS = [(mp, i) for mp in range(2) for k in range(HB) for i in (HB + k, k)]
    NI = len(ITEMS)
    ITEM_AT = [0, 2, 4, 6, 8, 10, 12, 14, 16, 18, 19, 20, 21, 22, 23, 23]
    LAG = 5
    PV1_AT = {min(at_st[1, j] + LAG - 1, NST - 1): j for j in range(SB)}
    PV0_AT = {1 + j: j for j in range(HB)}
    END1_AT, END0_AT = 1, 12
    with ExitStack() as ctx:
        m = Mem(nc, ctx, "att")
        ops = m.sb("ops", [KR + 3, SL, MATS, S], BF16)
        va = m.sb("va", [P, SL, SB, VC])
        pr = [m.sb("p0", [P, 2, HB, GN]), m.sb("p1", [P, 2, SB, GN])]
        mcol = m.sb("mcol", [P, 2 * SB])
        mneg = m.sb("mneg", [2 * SB, 2, P])
        mpart = m.sb("mpart", [2 * SB, 3, P], BF16)
        ot = [m.sb("ot0", [OW, GN]), m.sb("ot1", [OW, GN])]
        rl = m.sb("rl", [P, HB, 2])
        o12 = m.sb("o12", [P, 2, HB, VD])
        ofin = m.sb("ofin", [P, 2, SB, VD])
        smax = [m.ps("smax_s"), m.ps("smax_b", (P, 1024))]
        tp = m.ps("tp")
        stp = [m.ps(f"st{i}") for i in range(2)]
        op = [m.ps(f"pv{i}") for i in range(2)]
        loaded, max_placed, o_stored = m.sems("loaded", SL), m.sems("max_placed", SL), m.sems("o_stored", 2)
        pv_done, o_copied = m.sems("pv_done", 2), m.sems("o_copied", 2)
        (ones_set, sm_ready, sm_reduced, mt_ready, mt_chain, mt_read, mp_ready, st_ready, exp_done, masked,
         ot_ready, ot_read, nchain, head_ready, rows_set) = (m.sem(n) for n in (
             "ones_set", "sm_ready", "sm_reduced", "mt_ready", "mt_chain", "mt_read", "mp_ready", "st_ready", "exp_done",
             "masked", "ot_ready", "ot_read", "nchain", "head_ready", "rows_set"))
        pd = parts.rearrange("k m (t d) n -> t k m d n", d=D)
        LOADS = 16 * (2 * len(PAIRS) + 1)
        PLACED = 16 * 3

        block = ctx.enter_context(nc.Block())

        @block.sync
        def _(sp):
            def load(t, s):
                for n, (a, b) in enumerate(PAIRS):
                    for side, part in ((0, a), (2, b)):
                        one = pd[t:t + 1, part, side:side + 2] if isinstance(t, int) else pd[bass.ds(t, 1), part, side:side + 2]
                        sp.dma_start(ops[n * D:(n + 1) * D, s, side:side + 2, :],
                                     one.rearrange("a m d n -> (a d) m n")).then_inc(loaded[s], 16)
                sp.dma_start(va[:, s].rearrange("p t v -> p (t v)"), at(values, t)).then_inc(loaded[s], 16)

            def place(t, s):
                sp.wait_ge(mp_ready, t + 1)
                for k in range(3):
                    sp.dma_start(ops[KR + k:KR + k + 1, s, 0:2, :], mpart[:, k, :]).then_inc(max_placed[s], 16)

            def store(t, q):
                sp.wait_ge(head_ready, 2 * (t + 1))
                sp.dma_start(at(heads, t), ofin[:, q].rearrange("p b v -> p (b v)")).then_inc(o_stored[q], 16)

            def body(t, i, r, left):
                if left >= 1:
                    place(t + 1, (r + 1) % SL)
                if left >= 3:
                    wait_pos(sp, pv_done[0], t)
                    load(t + 3, (r + 3) % SL)
                if not isinstance(t, int) or t:
                    store(t - 1, (r - 1) % 2)

            for t in range(3):
                load(t, t)
            sp.wait_ge(ones_set, 1)
            place(0, 0)
            turns(sp, T, SL, body)
            store(T - 1, (T - 1) % 2)
            for r in range(2):
                sp.wait_ge(o_stored[r], 16 * (T // 2))

        @block.tensor
        def _(pe):
            def max_item(t, s, n):
                mp, i = ITEMS[n]
                wait_pos(pe, sm_reduced, t * NI + n - 1)
                out, w = smax[i >= HB], (i + 1) * P
                for c in range(0, w, GN):
                    k = min(GN, w - c)
                    nc.tensor.matmul(out[:, c:c + k], ops[0:KR, s, mp, i * P:w], ops[0:KR, s, 2 + mp, c:c + k],
                                     start=True, stop=(c + k < w))
                nc.tensor.matmul(out[:, i * P:w], C["identb"][:], C["mask"][:], start=False, stop=True)\
                    .then_inc(sm_ready, 1)

            def max_rows(t):
                pe.wait_ge(sm_reduced, (t + 1) * NI)
                nc.tensor.transpose(tp[0:2 * SB, 0:P], mcol[:], C["ident"][:]).then_inc(mt_ready, 1)

            def scores(t, s, n):
                half, j, mp, off = ST[n]
                wait_pos(pe, exp_done, t * NST + n - 1)
                nc.tensor.matmul(stp[n % 2][:, off:GN], ops[:, s, 2 + mp, j * P:(j + 1) * P],
                                 ops[:, s, mp, half * GN + off:(half + 1) * GN], start=True, stop=True).then_inc(st_ready, 1)

            def pv(t, s, half, j):
                last = HB * (half + 1) - 1
                if j == 0:
                    wait_pos(pe, o_copied[half], t)
                pe.wait_ge(exp_done, t * NST + at_st[half, j] + 1)
                off = max(0, j - HB * half) * P
                if j >= HB * half:
                    pe.wait_ge(masked, t * NSEL + (1 - half) * 2 * HB + 2 * (j - HB * half + 1))
                for mp in range(2):
                    ins = nc.tensor.matmul(op[half][mp * MB:mp * MB + VC, off:GN], va[:, s, j, :], pr[half][:, mp, j, off:GN],
                                           start=(j == 0), stop=(j == last))
                if j == last:
                    ins.then_inc(pv_done[half], 1)

            def end(t, half, mt):
                pe.wait_ge(o_copied[half], t + 1)
                wait_pos(pe, ot_read, 2 * t + (1 - half))
                if mt:
                    pe.wait_ge(mt_read, t + 3)
                for b in range(HB):
                    ins = nc.tensor.transpose(tp[:, b * OW:(b + 1) * OW], ot[half][:, b * P:(b + 1) * P], C["ident"][0:OW, 0:OW])
                ins.then_inc(ot_ready, 1)

            def body(t, i, r, left):
                s, s1, s2 = r, (r - 1) % SL, (r + 2) % SL
                first = isinstance(t, int) and t == 0
                pe.wait_ge(max_placed[s], PLACED * (i + 1))
                if left >= 2:
                    pe.wait_ge(loaded[s2], LOADS * (i + 1 + (r >= 2)))
                for n in range(NST):
                    scores(t, s, n)
                    if n == 0 and left >= 1:
                        wait_pos(pe, ot_read, 2 * (t - 1))
                        max_rows(t + 1)
                    if not first and n == END1_AT:
                        end(t - 1, 1, left >= 1)
                    if not first and n in PV0_AT:
                        pv(t - 1, s1, 0, PV0_AT[n])
                    if not first and n == END0_AT:
                        end(t - 1, 0, False)
                    if n in PV1_AT:
                        pv(t, s, 1, PV1_AT[n])
                    if left >= 2:
                        for k in range(NI):
                            if ITEM_AT[k] == n:
                                max_item(t + 2, s2, k)

            pe.wait_ge(rows_set, 2)
            pe.wait_ge(loaded[0], LOADS)
            for n in range(NI):
                max_item(0, 0, n)
            max_rows(0)
            pe.wait_ge(loaded[1], LOADS)
            pe.wait_ge(mt_read, 1)
            for n in range(NI):
                max_item(1, 1, n)
            turns(pe, T, SL, body)
            end(T - 1, 1, False)
            for j in range(HB):
                pv(T - 1, (T - 1) % SL, 0, j)
            end(T - 1, 0, False)

        @block.scalar
        def _(act):
            def copy_o(t, half):
                act.wait_ge(pv_done[half], t + 1)
                wait_pos(act, ot_ready, 2 * t - half)
                act.activation(ot[half][:], op[half][0:OW, :], ACT.Copy).then_inc(o_copied[half], 1)

            def body(t, i, r, left):
                for n, (half, j, mp, off) in enumerate(ST):
                    if j == 0 and mp == 0:
                        wait_pos(act, pv_done[half], t)
                    act.wait_ge(st_ready, t * NST + n + 1)
                    act.activation(pr[half][:, mp, j, off:GN], stp[n % 2][:, off:GN], ACT.Exp, scale=SCALE).then_inc(exp_done, 1)
                    if n == COPY0_AT and not (isinstance(t, int) and t == 0):
                        copy_o(t - 1, 0)
                copy_o(t, 1)

            COPY0_AT = 7
            turns(act, T, SL, body)
            copy_o(T - 1, 0)

        @block.gpsimd
        def _(pool):
            pool.memset(ops[KR:KR + 3, :, :, :].rearrange("p s m n -> p (s m n)"), 1.0).then_inc(ones_set, 1)

            def body(t, i, r, left):
                for n, (half, j, mp, off) in enumerate(ST):
                    if j >= HB * half:
                        wait_apart(pool, ones_set, exp_done, t * NST + n + 1)
                        d = pr[half][:, mp, j, off:off + P]
                        pool.affine_select(out=d, in_=d, compare_op=ALU.is_ge, fill=0.0, base=0,
                                           pattern=[[1, P]], channel_multiplier=-1).then_inc(masked, 1)

            turns(pool, T, SL, body)

        @block.vector
        def _(v):
            for half in range(2):
                v.memset(op[half][32:64, :], 0.0).then_inc(rows_set, 1)
            mc = Chain(v, mt_chain, 3)
            nch = Chain(v, nchain, 3)

            def reduce_item(t, n):
                mp, i = ITEMS[n]
                v.wait_ge(sm_ready, t * NI + n + 1)
                v.tensor_reduce(mcol[:, mp * SB + i:mp * SB + i + 1], smax[i >= HB][:, 0:(i + 1) * P], AX.X, ALU.max)\
                    .then_inc(sm_reduced, 1)

            def max_parts(t, s, uses):
                mc.turn(t)
                v.wait_ge(mt_ready, t + 1)
                v.tensor_scalar(mneg[:, 0], tp[0:2 * SB, 0:P], -1.0, None, ALU.mult).then_inc(mt_read, 1)
                v.wait_ge(mt_read, t + 1)
                if not isinstance(uses, int) or uses:
                    v.wait_ge(max_placed[s], PLACED * uses)
                mc.link(v.tensor_copy(mpart[:, 0], mneg[:, 0]))
                mc.link(v.tensor_tensor(mneg[:, 1], mneg[:, 0], mpart[:, 0], ALU.subtract))
                mc.link(v.tensor_copy(mpart[:, 1], mneg[:, 1]))
                v.tensor_tensor(mpart[:, 2], mneg[:, 1], mpart[:, 1], ALU.subtract).then_inc(mp_ready, 1)

            def norm(t, q, uses, half):
                k = 2 * t + (1 - half)
                nch.turn(k)
                v.wait_ge(ot_ready, k + 1)
                o = tp[:, 0:HB * OW].rearrange("p (b w) -> p b w", b=HB)
                nch.link(v.reciprocal(rl[:], o[:, :, VD:OW:MB]))
                lam = C["neglam"][:, t:t + 1] if isinstance(t, int) else C["neglam"][:, bass.ds(t, 1)]
                nch.mark(v.tensor_tensor(o12[:, 0], o[:, :, 0:VD], bcast(rl[:, :, 0:1], [P, HB, VD]), ALU.mult))
                nch.link(v.tensor_scalar(rl[:, :, 1], rl[:, :, 1], lam, None, ALU.mult))
                v.tensor_tensor(o12[:, 1], o[:, :, MB:MB + VD], bcast(rl[:, :, 1:2], [P, HB, VD]), ALU.mult).then_inc(ot_read, 1)
                v.wait_ge(ot_read, k + 1)
                wait_pos(v, o_stored[q], 16 * uses)
                v.tensor_tensor(ofin[:, q, half * HB:(half + 1) * HB], o12[:, 0], o12[:, 1], ALU.add).then_inc(head_ready, 1)

            def body(t, i, r, left):
                if left >= 1:
                    max_parts(t + 1, r, i + 1)
                for n in range(NI):
                    if left >= 2:
                        reduce_item(t + 2, n)
                    if n in NORM_AT and not (isinstance(t, int) and t == 0):
                        norm(t - 1, (r - 1) % 2, 2 * i + (r - 1) // 2, NORM_AT[n])

            NORM_AT = {1: 1, 6: 0}
            for n in range(NI):
                reduce_item(0, n)
            max_parts(0, 0, 0)
            for n in range(NI):
                reduce_item(1, n)
            turns(v, T, SL, body)
            for half in (1, 0):
                norm(T - 1, (T - 1) % 2, (T - 1) // 2, half)


class Power:

    def __init__(self, m, C):
        self.asked, self.told, self.C = m.sem("var_ready"), m.sem("rstd_ready"), C

    def ask(self, v, ins, k):
        ins.then_inc(self.asked, 1)
        v.wait_ge(self.told, k + 1)

    def serve(self, nc, pool, var, rstd, k):
        pool.wait_ge(self.asked, k + 1)
        nc.gpsimd.tensor_tensor(rstd, var, self.C["neghalf"][:, 0:var.shape[1]], ALU.pow).then_inc(self.told, 1)


def merge_and_ffn(nc, I, C, heads, x_in, x_out):
    HC = H * VD // P
    with ExitStack() as ctx:
        m = Mem(nc, ctx, "ffn")
        os_ = m.sb("os", [P, 2, H, GT, VD])
        xs = m.sb("xs", [P, 2, GT, E])
        xc, sq = m.sb("xc", [P, H * GT, VD]), m.sb("sq", [P, H * GT, VD])
        hm, hv, hr = m.sb("hm", [P, H * GT]), m.sb("hv", [P, H * GT]), m.sb("hr", [P, H * GT])
        on, mt = m.sb("on", [P, GT, H * VD]), m.sb("mt", [P, HC, GN])
        x1, xn, xt = m.sb("x1", [P, 2, GT, E]), m.sb("xn", [P, GT, E]), m.sb("xt", [P, EC, GN])
        ht = m.sb("ht", [P, FM, GN])
        yb, yn, xo = m.sb("yb", [P, GT, E]), m.sb("yn", [P, GT, E]), m.sb("xo", [P, 2, GT, E])
        stats, mv = m.sb("stats", [P, GT, 6]), m.sb("mv", [P, GT, 2])
        var, rstd = m.sb("var", [P, GT]), m.sb("rstd", [P, GT])
        tp, hp, ya, yo = ([m.ps(f"{n}{i}") for i in range(2)] for n in ("tp", "hp", "ya", "yo"))
        h_loaded, x_loaded, x_stored = m.sems("h_loaded", 2), m.sems("x_loaded", 2), m.sems("x_stored", 2)
        (hc, centred, squared, on_ready, tp_ready, tp_copied, ya_ready, ya_read, yo_ready, yo_read, s1, s2, s3, x1_ready,
         xn_ready, hid_ready, gelu_done, out_ready, c3) = (m.sem(n) for n in (
             "hc", "centred", "squared", "on_ready", "tp_ready", "tp_copied", "ya_ready", "ya_read", "yo_ready", "yo_read",
             "s1", "s2", "s3", "x1_ready", "xn_ready", "hid_ready", "gelu_done", "out_ready", "c3"))
        power = Power(m, C)
        hg = heads.rearrange("(b h) p (c w) -> b c p h w", b=B, c=GB)
        xg = x_in.rearrange("(g t p) e -> g p t e", p=P, t=GT)
        og = x_out.rearrange("(g t p) e -> g p t e", p=P, t=GT)
        NTP = HC + EC
        block = ctx.enter_context(nc.Block())

        @block.sync
        def _(sp):
            def load(g, i, r):
                sp.dma_start(os_[:, r].rearrange("p h t v -> p h (t v)"), at(hg[:, r], i)).then_inc(h_loaded[r], 16)
                sp.dma_start(xs[:, r], at(xg, g)).then_inc(x_loaded[r], 16)

            def body(g, i, r, left):
                sp.wait_ge(x1_ready, g + 1)
                if left >= 2:
                    load(g + 2, i + 1, r)
                sp.wait_ge(out_ready, g + 1)
                sp.dma_start(at(og, g), xo[:, r]).then_inc(x_stored[r], 16)

            for g in range(2):
                load(g, 0, g)
            turns(sp, G, 2, body)
            for r in range(2):
                sp.wait_ge(x_stored[r], 16 * (G // 2 + 1))

        @block.gpsimd
        def _(pool):
            def serve_a(k):
                power.serve(nc, pool, hv[:], hr[:], k)
                power.serve(nc, pool, var[:], rstd[:], k + 1)
                power.serve(nc, pool, var[:], rstd[:], k + 2)

            def body(g, i, r, left):
                if left:
                    serve_a(3 + 4 * g)
                power.serve(nc, pool, var[:], rstd[:], 3 + 4 * g + (3 if left else 0))

            serve_a(0)
            turns(pool, G, 2, body)

        @block.tensor
        def _(pe):
            pe.wait_ge(C["s_ffn"], 48)

            def transposed(src, n):
                pass

            def merge(g, base):
                pe.wait_ge(on_ready, g + 1)
                for c in range(HC):
                    wait_pos(pe, tp_copied, base + c - 1)
                    for t in range(GT):
                        ins = nc.tensor.transpose(tp[c % 2][:, t * P:(t + 1) * P], on[:, t, c * P:(c + 1) * P], C["ident"][:])
                    ins.then_inc(tp_ready, 1)
                for t in range(GT):
                    pe.wait_ge(tp_copied, base + HC)
                    if t % 2 == 0:
                        wait_pos(pe, ya_read, g)
                    for c in range(HC):
                        ins = nc.tensor.matmul(ya[t // 2][:, t % 2 * E:(t % 2 + 1) * E], mt[:, c, t * P:(t + 1) * P],
                                               C["wo"][:, c], start=(c == 0), stop=(c == HC - 1))
                    ins.then_inc(ya_ready, 1)

            def turn_x(g, base):
                pe.wait_ge(xn_ready, g + 1)
                for c in range(EC):
                    pe.wait_ge(tp_copied, base + HC + c - 1)
                    for t in range(GT):
                        ins = nc.tensor.transpose(tp[c % 2][:, t * P:(t + 1) * P], xn[:, t, c * P:(c + 1) * P], C["ident"][:])
                    ins.then_inc(tp_ready, 1)

            def body(g, i, r, left):
                pe.wait_ge(tp_copied, (g + 1) * NTP)
                for n in range(FM):
                    pe.wait_ge(gelu_done, g * FM + n + 1)
                    for c in range(EC):
                        ins = nc.tensor.matmul(hp[n % 2][:], C["w1t"][:, c, n * P:(n + 1) * P], xt[:, c], start=(c == 0), stop=(c == EC - 1))
                    ins.then_inc(hid_ready, 1)
                if left:
                    merge(g + 1, (g + 1) * NTP)
                pe.wait_ge(gelu_done, (g + 1) * FM + 2)
                for t in range(GT):
                    if t % 2 == 0:
                        wait_pos(pe, yo_read, 2 * g - 1 + t // 2)
                    for n in range(FM):
                        ins = nc.tensor.matmul(yo[t // 2][:, t % 2 * E:(t % 2 + 1) * E], ht[:, n, t * P:(t + 1) * P],
                                               C["w2t"][:, n], start=(n == 0), stop=(n == FM - 1))
                    ins.then_inc(yo_ready, 1)
                if left:
                    turn_x(g + 1, (g + 1) * NTP)

            merge(0, 0)
            turn_x(0, 0)
            turns(pe, G, 2, body)

        @block.scalar
        def _(act):
            act.sem_inc(gelu_done, 2)

            def group(g, base):
                act.wait_ge(centred, g + 1)
                act.activation(sq[:], xc[:], ACT.Square).then_inc(squared, 1)
                for c in range(HC):
                    act.wait_ge(tp_ready, base + c + 1)
                    act.activation(mt[:, c], tp[c % 2][:], ACT.Copy).then_inc(tp_copied, 1)

            def x_group(base):
                for c in range(EC):
                    act.wait_ge(tp_ready, base + HC + c + 1)
                    act.activation(xt[:, c], tp[c % 2][:], ACT.Copy).then_inc(tp_copied, 1)

            def body(g, i, r, left):
                for n in range(FM):
                    act.wait_ge(hid_ready, g * FM + n + 1)
                    act.activation(ht[:, n], hp[n % 2][:], ACT.Gelu, bias=C["b1"][:, n:n + 1]).then_inc(gelu_done, 1)
                    if n == FM // 2 and left:
                        act.wait_ge(centred, g + 2)
                        act.activation(sq[:], xc[:], ACT.Square).then_inc(squared, 1)
                if left:
                    for c in range(HC):
                        act.wait_ge(tp_ready, (g + 1) * NTP + c + 1)
                        act.activation(mt[:, c], tp[c % 2][:], ACT.Copy).then_inc(tp_copied, 1)
                    x_group((g + 1) * NTP)

            group(0, 0)
            x_group(0)
            turns(act, G, 2, body)

        @block.vector
        def _(v):
            for r in range(2):
                v.sem_inc(x_stored[r], 16)
            hch, ach, bch, cch = Chain(v, hc, 4), Chain(v, s1, 3 * GT - 1), Chain(v, s2, 2 * GT), Chain(v, s3, 2 * GT + GT)

            def head_norm(g, r, uses, k):
                hch.turn(g)
                v.wait_ge(h_loaded[r], 16 * uses)
                src = os_[:, r].rearrange("p h t v -> p (h t) v")
                shape = [P, H * GT, VD]
                hch.link(v.tensor_reduce(hm[:], src, AX.X, ALU.add))
                hch.link(v.tensor_scalar(hm[:], hm[:], 1.0 / VD, None, ALU.mult))
                v.tensor_tensor(xc[:], src, bcast(hm[:].unsqueeze(2), shape), ALU.subtract).then_inc(centred, 1)
                v.wait_ge(squared, g + 1)
                hch.link(v.tensor_reduce(hv[:], sq[:], AX.X, ALU.add))
                power.ask(v, v.tensor_scalar(hv[:], hv[:], 1.0 / VD, EPS, ALU.mult, ALU.add), k)
                hch.link(v.tensor_scalar(hr[:], hr[:], 1.0 - LAM_INIT, None, ALU.mult))
                dst = on[:].rearrange("p t (h v) -> p h t v", h=H)
                hrv = hr[:].rearrange("p (h t) -> p h t", h=H)
                for t in range(GT):
                    ins = v.tensor_tensor(dst[:, :, t], xc[:].rearrange("p (h t) v -> p h t v", h=H)[:, :, t],
                                          bcast(hrv[:, :, t:t + 1], [P, H, VD]), ALU.mult)
                ins.then_inc(on_ready, 1)

            def merged(g, r, uses, k):
                ach.turn(g)
                bch.turn(g)
                v.wait_ge(ya_ready, (g + 1) * GT)
                y = lambda t: ya[t // 2][:, t % 2 * E:(t % 2 + 1) * E]
                mean_var(v, ach, C["go"], y, stats, mv, GT)
                power.ask(v, v.tensor_scalar(var[:], mv[:, :, 1], EPS, None, ALU.add), k)
                for t in range(GT):
                    ins = v.tensor_scalar(yn[:, t], y(t), mv[:, t, 0:1], rstd[:, t:t + 1], ALU.subtract, ALU.mult)
                    if t == GT - 1:
                        ins.then_inc(ya_read, 1)
                    else:
                        ach.mark(ins)
                v.wait_ge(ya_read, g + 1)
                v.wait_ge(x_loaded[r], 16 * uses)
                v.tensor_tensor(x1[:, r], xs[:, r], yn[:], ALU.add).then_inc(x1_ready, 1)
                v.wait_ge(x1_ready, g + 1)
                mean_var(v, bch, C["go"], lambda t: x1[:, r, t], stats, mv, GT)
                power.ask(v, v.tensor_scalar(var[:], mv[:, :, 1], EPS, None, ALU.add), k + 1)
                for t in range(GT):
                    ins = v.tensor_scalar(xn[:, t], x1[:, r, t], mv[:, t, 0:1], rstd[:, t:t + 1], ALU.subtract, ALU.mult)
                ins.then_inc(xn_ready, 1)

            def finish(g, i, r, k):
                cch.turn(g)
                wait_pos(v, out_ready, g)
                for n in range(2):
                    v.wait_ge(yo_ready, g * GT + 2 * n + 2)
                    v.tensor_tensor(yb[:, 2 * n:2 * n + 2], yo[n][:].rearrange("p (t e) -> p t e", t=2),
                                    bcast(C["b2"][:].unsqueeze(1), [P, 2, E]), ALU.add).then_inc(yo_read, 1)
                v.wait_ge(yo_read, 2 * g + 2)
                mean_var(v, cch, C["go"], lambda t: yb[:, t], stats, mv, GT)
                power.ask(v, v.tensor_scalar(var[:], mv[:, :, 1], EPS, None, ALU.add), k)
                for t in range(GT):
                    cch.mark(v.tensor_scalar(yb[:, t], yb[:, t], mv[:, t, 0:1], rstd[:, t:t + 1], ALU.subtract, ALU.mult))
                v.wait_ge(x_stored[r], 16 * (i + 1))
                cch.wait()
                v.tensor_tensor(xo[:, r], x1[:, r], yb[:], ALU.add).then_inc(out_ready, 1)

            def body(g, i, r, left):
                if left:
                    head_norm(g + 1, (r + 1) % 2, i + 1 + r, 3 + 4 * g)
                    merged(g + 1, (r + 1) % 2, i + 1 + r, 3 + 4 * g + 1)
                finish(g, i, r, 3 + 4 * g + (3 if left else 0))

            head_norm(0, 0, 1, 0)
            merged(0, 0, 1, 1)
            turns(v, G, 2, body)


def convolve(nc, I, C, x_in, x_out):
    NT = 5
    TILES = [(c, h) for c in range(EC) for h in range(GB)]
    NTL = len(TILES)
    with ExitStack() as ctx:
        m = Mem(nc, ctx, "cnv")
        xs, xn = m.sb("xs", [P, 2, SB, E]), m.sb("xn", [P, SB, E])
        xt = m.sb("xt", [P, EC, S])
        sg = m.sb("sg", [P, EC, S])
        gp = m.sb("gp", [P, EC, S + 2 * PAD])
        acc = m.sb("acc", [P, EC, S])
        dg = m.sb("dg", [P, EC, NT, P])
        yb, xo = m.sb("yb", [P, SB, E]), m.sb("xo", [P, 2, SB, E])
        stats, mv, var, rstd = m.sb("stats", [P, SB, 6]), m.sb("mv", [P, SB, 2]), m.sb("var", [P, SB]), m.sb("rstd", [P, SB])
        tp, tap, yo = ([m.ps(f"{n}{i}") for i in range(2)] for n in ("tp", "tap", "yo"))
        ap, gpp = m.ps("a"), m.ps("g")
        x_loaded, x_stored = m.sems("x_loaded", 2), m.sems("x_stored", 2)
        (edges, s1, s2, s3, xn_ready, tp_ready, tp_copied, a_ready, g_ready, sig_done, glu_done, taps_ready, taps_read,
         acc_ready, yo_ready, yo_read, out_ready) = (m.sem(n) for n in (
             "edges", "s1", "s2", "s3", "xn_ready", "tp_ready", "tp_copied", "a_ready", "g_ready", "sig_done", "glu_done",
             "taps_ready", "taps_read", "acc_ready", "yo_ready", "yo_read", "out_ready"))
        power = Power(m, C)
        xg = x_in.rearrange("(b t p) e -> b p t e", p=P, t=SB)
        og = x_out.rearrange("(b t p) e -> b p t e", p=P, t=SB)
        block = ctx.enter_context(nc.Block())

        @block.sync
        def _(sp):
            def body(b, i, r, left):
                sp.wait_ge(out_ready, b + 1)
                sp.dma_start(at(og, b), xo[:, r]).then_inc(x_stored[r], 16)
                if left >= 2:
                    sp.dma_start(xs[:, r], at(xg, b + 2)).then_inc(x_loaded[r], 16)

            for b in range(2):
                sp.dma_start(xs[:, b], at(xg, b)).then_inc(x_loaded[b], 16)
            turns(sp, B, 2, body)
            for r in range(2):
                sp.wait_ge(x_stored[r], 16 * (B // 2 + 1))

        @block.gpsimd
        def _(pool):
            def body(b, i, r, left):
                if left:
                    power.serve(nc, pool, var[:], rstd[:], 1 + 2 * b)
                power.serve(nc, pool, var[:], rstd[:], 1 + 2 * b + (1 if left else 0))

            power.serve(nc, pool, var[:], rstd[:], 0)
            turns(pool, B, 2, body)

        @block.tensor
        def _(pe):
            pe.wait_ge(C["s_conv"], 64)
            pe.wait_ge(edges, 2 + EC * NT)

            def gates(b):
                pe.wait_ge(xn_ready, b + 1)
                for n, (c, h) in enumerate(TILES):
                    wait_pos(pe, tp_copied, b * NTL + n - 1)
                    for t in range(GT):
                        ins = nc.tensor.transpose(tp[n % 2][:, t * P:(t + 1) * P], xn[:, h * GT + t, c * P:(c + 1) * P], C["ident"][:])
                    ins.then_inc(tp_ready, 1)
                pe.wait_ge(tp_copied, (b + 1) * NTL)
                for n, (c, h) in enumerate(TILES):
                    for dst, ready, read, col in ((gpp, g_ready, sig_done, E), (ap, a_ready, glu_done, 0)):
                        wait_pos(pe, read, b * NTL + n)
                        for k in range(EC):
                            ins = nc.tensor.matmul(dst[:], C["cw1"][:, k, col + c * P:col + (c + 1) * P],
                                                   xt[:, k, h * GN:(h + 1) * GN], start=(k == 0), stop=(k == EC - 1))
                        ins.then_inc(ready, 1)

            def body(b, i, r, left):
                pe.wait_ge(glu_done, (b + 1) * NTL)
                for n, (c, h) in enumerate(TILES):
                    wait_pos(pe, taps_read, b * NTL + n - 1)
                    for k in range(NT):
                        ins = nc.tensor.matmul(tap[n % 2][:], dg[:, c, k], gp[:, c, h * GN + k:(h + 1) * GN + k],
                                               start=(k == 0), stop=(k == NT - 1))
                    ins.then_inc(taps_ready, 1)
                if left:
                    gates(b + 1)
                pe.wait_ge(acc_ready, (b + 1) * NTL)
                for t in range(SB):
                    if t % 2 == 0:
                        wait_pos(pe, yo_read, b * (SB // 2) + t // 2 - 1)
                    for c in range(EC):
                        ins = nc.tensor.matmul(yo[t // 2 % 2][:, t % 2 * E:(t % 2 + 1) * E], acc[:, c, t * P:(t + 1) * P],
                                               C["cw2"][:, c], start=(c == 0), stop=(c == EC - 1))
                    ins.then_inc(yo_ready, 1)

            gates(0)
            turns(pe, B, 2, body)

        @block.scalar
        def _(act):
            def gates(b):
                for n, (c, h) in enumerate(TILES):
                    act.wait_ge(tp_ready, b * NTL + n + 1)
                    act.activation(xt[:, c, h * GN:(h + 1) * GN], tp[n % 2][:], ACT.Copy).then_inc(tp_copied, 1)
                wait_pos(act, glu_done, b * NTL)
                for n, (c, h) in enumerate(TILES):
                    act.wait_ge(g_ready, b * NTL + n + 1)
                    act.activation(sg[:, c, h * GN:(h + 1) * GN], gpp[:], ACT.Sigmoid, bias=C["cb1"][:, EC + c:EC + c + 1])\
                        .then_inc(sig_done, 1)

            gates(0)
            turns(act, B, 2, lambda b, i, r, left: gates(b + 1) if left else None)

        @block.vector
        def _(v):
            for r in range(2):
                v.sem_inc(x_stored[r], 16)
            v.wait_ge(C["s_conv"], 64)
            v.memset(gp[:, :, 0:PAD], 0.0).then_inc(edges, 1)
            v.memset(gp[:, :, PAD + S:], 0.0).then_inc(edges, 1)
            for c in range(EC):
                for k in range(NT):
                    v.tensor_scalar(dg[:, c, k], C["ident"][:], C["filt"][:, c, k:k + 1], None, ALU.mult).then_inc(edges, 1)
            v.wait_ge(edges, 2 + EC * NT)
            pch, tch, ych = Chain(v, s1, 2 * SB), Chain(v, s2, (K - NT - 2) * NTL), Chain(v, s3, 3 * SB)

            def pre(b, r, uses, k):
                pch.turn(b)
                v.wait_ge(x_loaded[r], 16 * uses)
                mean_var(v, pch, C["go"], lambda t: xs[:, r, t], stats, mv, SB)
                power.ask(v, v.tensor_scalar(var[:], mv[:, :, 1], EPS, None, ALU.add), k)
                for t in range(SB):
                    ins = v.tensor_scalar(xn[:, t], xs[:, r, t], mv[:, t, 0:1], rstd[:, t:t + 1], ALU.subtract, ALU.mult)
                ins.then_inc(xn_ready, 1)

            def glu(b):
                wait_pos(v, acc_ready, b * NTL)
                for n, (c, h) in enumerate(TILES):
                    v.wait_ge(a_ready, b * NTL + n + 1)
                    v.wait_ge(sig_done, b * NTL + n + 1)
                    v.scalar_tensor_tensor(out=gp[:, c, PAD + h * GN:PAD + (h + 1) * GN], in0=ap[:], scalar=C["cb1"][:, c:c + 1],
                                           in1=sg[:, c, h * GN:(h + 1) * GN], op0=ALU.add, op1=ALU.mult).then_inc(glu_done, 1)

            def body(b, i, r, left):
                if left:
                    pre(b + 1, (r + 1) % 2, i + 1 + r, 1 + 2 * b)
                tch.turn(b)
                v.wait_ge(glu_done, (b + 1) * NTL)
                for k in range(NT, K):
                    for n, (c, h) in enumerate(TILES):
                        a = acc[:, c, h * GN:(h + 1) * GN]
                        if k == NT:
                            v.wait_ge(taps_ready, b * NTL + n + 1)
                        elif k == NT + 1:
                            v.wait_ge(taps_read, b * NTL + n + 1)
                        else:
                            v.wait_ge(s2, tch.base + (k - NT - 2) * NTL + n + 1)
                        ins = v.scalar_tensor_tensor(out=a, in0=gp[:, c, h * GN + k:(h + 1) * GN + k],
                                                     scalar=C["filt"][:, c, k:k + 1], in1=tap[n % 2][:] if k == NT else a,
                                                     op0=ALU.mult, op1=ALU.add)
                        if k == NT:
                            ins.then_inc(taps_read, 1)
                        elif k == K - 1:
                            ins.then_inc(acc_ready, 1)
                        else:
                            tch.mark(ins)
                if left:
                    glu(b + 1)
                ych.turn(b)
                wait_pos(v, out_ready, b)
                for n in range(SB // 2):
                    v.wait_ge(yo_ready, b * SB + 2 * n + 2)
                    v.tensor_tensor(yb[:, 2 * n:2 * n + 2], yo[n % 2][:].rearrange("p (t e) -> p t e", t=2),
                                    bcast(C["cb2"][:].unsqueeze(1), [P, 2, E]), ALU.add).then_inc(yo_read, 1)
                v.wait_ge(yo_read, (b + 1) * (SB // 2))
                mean_var(v, ych, C["go"], lambda t: yb[:, t], stats, mv, SB)
                power.ask(v, v.tensor_scalar(var[:], mv[:, :, 1], EPS, None, ALU.add), 1 + 2 * b + (1 if left else 0))
                for t in range(SB):
                    ych.mark(v.tensor_scalar(yb[:, t], yb[:, t], mv[:, t, 0:1], rstd[:, t:t + 1], ALU.subtract, ALU.mult))
                v.wait_ge(x_stored[r], 16 * (i + 1))
                ych.wait()
                v.tensor_tensor(xo[:, r], xs[:, r], yb[:], ALU.add).then_inc(out_ready, 1)

            pre(0, 0, 1, 0)
            glu(0)
            turns(v, B, 2, body)


def experts(nc, I, C, x_in, x_out):
    NEXT_AT = 9
    with ExitStack() as ctx:
        m = Mem(nc, ctx, "moe")
        xs, xn, xt = m.sb("xs", [P, 2, GT, E]), m.sb("xn", [P, GT, E]), m.sb("xt", [P, 2, EC, GN])
        si, hh = m.sb("si", [P, 2, GN]), m.sb("hh", [P, 2, GN])
        comb, combt = m.sb("comb", [P, 2, GT, NX]), m.sb("combt", [NE, 2, GN])
        ya, yb, xo = m.sb("ya", [P, GT, E]), m.sb("yb", [P, GT, E]), m.sb("xo", [P, 2, GT, E])
        stats, mv, var, rstd = m.sb("stats", [P, GT, 6]), m.sb("mv", [P, GT, 2]), m.sb("var", [P, GT]), m.sb("rstd", [P, GT])
        lg, ex, sc = m.sb("lg", [P, GT, NE]), m.sb("ex", [P, GT, NE]), m.sb("sc", [P, GT, NE])
        mx, sm = m.sb("mx", [P, GT]), m.sb("sm", [P, GT])
        pairs = m.sb("pairs", [P, GT * NG, 6])
        gs = m.sb("gs", [P, GT, NG])
        g1, g2, gr = m.sb("g1", [P, GT, NG, NG]), m.sb("g2", [P, GT, NG, NG]), m.sb("gr", [P, GT, NG])
        pen = m.sb("pen", [P, GT, NG])
        e1, e2, er = m.sb("e1", [P, GT, NE, NE]), m.sb("e2", [P, GT, NE, NE]), m.sb("er", [P, GT, NE])
        h1, h3, yp = ([m.ps(f"{n}{i}") for i in range(2)] for n in ("h1", "h3", "y"))
        tp = [m.ps(f"tp{i}") for i in range(2)]
        x_loaded, x_stored = m.sems("x_loaded", 2), m.sems("x_stored", 2)
        (s1, s3, xn_ready, tp_ready, xt_ready, lg_ready, lg_read, lg_shift, exp_done, rch, comb_ready, ct_ready, ct_copied,
         be_ready, be_read, h1_ready, h3_ready, silu_done, h_done, y_ready, y_read, out_ready, c18) = (m.sem(n) for n in (
             "s1", "s3", "xn_ready", "tp_ready", "xt_ready", "lg_ready", "lg_read", "lg_shift", "exp_done", "rch",
             "comb_ready", "ct_ready", "ct_copied", "be_ready", "be_read", "h1_ready", "h3_ready", "silu_done", "h_done",
             "y_ready", "y_read", "out_ready", "c18"))
        power = Power(m, C)
        xg = x_in.rearrange("(g t p) e -> g p t e", p=P, t=GT)
        og = x_out.rearrange("(g t p) e -> g p t e", p=P, t=GT)
        block = ctx.enter_context(nc.Block())

        @block.sync
        def _(sp):
            def body(g, i, r, left):
                sp.wait_ge(out_ready, g + 1)
                sp.dma_start(at(og, g), xo[:, r]).then_inc(x_stored[r], 16)
                if left >= 2:
                    sp.dma_start(xs[:, r], at(xg, g + 2)).then_inc(x_loaded[r], 16)

            for g in range(2):
                sp.dma_start(xs[:, g], at(xg, g)).then_inc(x_loaded[g], 16)
            turns(sp, G, 2, body)
            for r in range(2):
                sp.wait_ge(x_stored[r], 16 * (G // 2 + 1))

        @block.gpsimd
        def _(pool):
            pool.memset(comb[:, :, :, NE:NX].rearrange("p s t e -> p (s t) e"), 1.0).then_inc(c18, 1)

            def body(g, i, r, left):
                if left:
                    power.serve(nc, pool, var[:], rstd[:], 1 + 2 * g)
                power.serve(nc, pool, var[:], rstd[:], 1 + 2 * g + (1 if left else 0))

            power.serve(nc, pool, var[:], rstd[:], 0)
            turns(pool, G, 2, body)

        @block.tensor
        def _(pe):
            pe.wait_ge(C["s_moe"], C["n_moe"])

            def inputs(g, r):
                pe.wait_ge(xn_ready, g + 1)
                wait_pos(pe, be_read, 2 * g)
                for c in range(EC):
                    for t in range(GT):
                        ins = nc.tensor.transpose(tp[c][:, t * P:(t + 1) * P], xn[:, t, c * P:(c + 1) * P], C["ident"][:])
                    ins.then_inc(tp_ready, 1)
                pe.wait_ge(xt_ready, (g + 1) * EC)
                for t in range(GT):
                    for c in range(EC):
                        ins = nc.tensor.matmul(tp[0][:, t * NE:(t + 1) * NE], xt[:, r, c, t * P:(t + 1) * P], C["gw"][:, c],
                                               start=(c == 0), stop=(c == EC - 1))
                ins.then_inc(lg_ready, 1)

            def routing(g, r):
                pe.wait_ge(comb_ready, g + 1)
                for t in range(GT):
                    ins = nc.tensor.transpose(tp[0][0:NE, t * P:(t + 1) * P], comb[:, r, t, 0:NE], C["ident"][:])
                ins.then_inc(ct_ready, 1)

            def hidden(g, r, x):
                n = g * NX + x
                for w, dst, ready, read in ((C["xw1"], h1, h1_ready, silu_done), (C["xw3"], h3, h3_ready, h_done)):
                    wait_pos(pe, read, n - 1)
                    for c in range(EC):
                        ins = nc.tensor.matmul(dst[x % 2][:], w[:, c, x], xt[:, r, c], start=(c == 0), stop=(c == EC - 1))
                    ins.then_inc(ready, 1)

            def down(g, x):
                n = g * NX + x
                pe.wait_ge(h_done, n + 1)
                for t in range(GT):
                    if t % 2 == 0:
                        wait_pos(pe, y_read, GT * n - 2 + t)
                    nc.tensor.matmul(yp[t // 2][:, t % 2 * E:(t % 2 + 1) * E], hh[:, x % 2, t * P:(t + 1) * P],
                                     C["xw2"][:, x], start=True, stop=True).then_inc(y_ready, 1)

            def biases(g, r, n):
                pe.wait_ge(ct_copied, g + 1)
                if n:
                    pe.wait_ge(be_read, 2 * g + 1)
                for t in (2 * n, 2 * n + 1):
                    ins = nc.tensor.matmul(tp[1][:, t % 2 * E:(t % 2 + 1) * E], combt[:, r, t * P:(t + 1) * P], C["xb2"][:],
                                           start=True, stop=True)
                ins.then_inc(be_ready, 1)

            def body(g, i, r, left):
                pe.wait_ge(xt_ready, (g + 1) * EC)
                for x in range(NX):
                    hidden(g, r, x)
                    if x == 1:
                        routing(g, r)
                    if x in (3, 5):
                        biases(g, r, (x - 3) // 2)
                    if x:
                        down(g, x - 1)
                    if x == NEXT_AT and left:
                        inputs(g + 1, (r + 1) % 2)
                down(g, NX - 1)

            inputs(0, 0)
            turns(pe, G, 2, body)

        @block.scalar
        def _(act):
            def inputs(g, r):
                for c in range(EC):
                    act.wait_ge(tp_ready, g * EC + c + 1)
                    act.activation(xt[:, r, c], tp[c][:], ACT.Copy).then_inc(xt_ready, 1)

            def exps(g):
                act.wait_ge(lg_shift, g + 1)
                act.activation(ex[:], lg[:], ACT.Exp).then_inc(exp_done, 1)

            def body(g, i, r, left):
                for x in range(NX):
                    n = g * NX + x
                    act.wait_ge(h1_ready, n + 1)
                    wait_pos(act, h_done, n - 1)
                    act.activation(si[:, x % 2], h1[x % 2][:], ACT.Silu, bias=C["xb1"][:, x:x + 1]).then_inc(silu_done, 1)
                    if x == 1:
                        act.wait_ge(ct_ready, g + 1)
                        act.activation(combt[:, r], tp[0][0:NE, :], ACT.Copy).then_inc(ct_copied, 1)
                    if x == NEXT_AT and left:
                        inputs(g + 1, (r + 1) % 2)
                    if x == NEXT_AT + 2 and left:
                        exps(g + 1)

            inputs(0, 0)
            exps(0)
            turns(act, G, 2, body)

        @block.vector
        def _(v):
            v.wait_ge(c18, 1)
            for r in range(2):
                v.sem_inc(x_stored[r], 16)
            pch, ych, rc = Chain(v, s1, 2 * GT), Chain(v, s3, 3 * GT), Chain(v, rch, 22)

            def pre(g, r, uses, k):
                pch.turn(g)
                v.wait_ge(x_loaded[r], 16 * uses)
                mean_var(v, pch, C["go"], lambda t: xs[:, r, t], stats, mv, GT)
                power.ask(v, v.tensor_scalar(var[:], mv[:, :, 1], EPS, None, ALU.add), k)
                for t in range(GT):
                    ins = v.tensor_scalar(xn[:, t], xs[:, r, t], mv[:, t, 0:1], rstd[:, t:t + 1], ALU.subtract, ALU.mult)
                ins.then_inc(xn_ready, 1)

            def shift(g):
                rc.turn(g)
                v.wait_ge(lg_ready, g + 1)
                logits = tp[0][:, 0:GT * NE].rearrange("p (t e) -> p t e", t=GT)
                rc.link(v.tensor_reduce(mx[:], logits, AX.X, ALU.max))
                v.tensor_tensor(lg[:], logits, bcast(mx[:].unsqueeze(2), [P, GT, NE]), ALU.subtract).then_inc(lg_shift, 1)

            def route(g, r):
                v.wait_ge(exp_done, g + 1)
                T3 = [P, GT, NE]
                rc.link(v.tensor_reduce(sm[:], ex[:], AX.X, ALU.add))
                rc.link(v.reciprocal(sm[:], sm[:]))
                rc.link(v.tensor_tensor(ex[:], ex[:], bcast(sm[:].unsqueeze(2), T3), ALU.mult))
                rc.link(v.tensor_tensor(sc[:], ex[:], C["gb"][:], ALU.add))
                s4 = sc[:].rearrange("p t (g e) -> p (t g) e", g=NG)
                rc.mark(v.tensor_tensor(pairs[:, :, 0:3], s4[:, :, 0:3], s4[:, :, 1:4], ALU.add))
                rc.mark(v.tensor_tensor(pairs[:, :, 3:5], s4[:, :, 0:2], s4[:, :, 2:4], ALU.add))
                rc.link(v.tensor_tensor(pairs[:, :, 5:6], s4[:, :, 0:1], s4[:, :, 3:4], ALU.add))
                rc.link(v.tensor_reduce(gs[:].rearrange("p t g -> p (t g)"), pairs[:], AX.X, ALU.max))

                def rank(val, n, one, two, out, tri):
                    shape = [P, GT, n, n]
                    other, own = bcast(val.unsqueeze(2), shape), bcast(val.unsqueeze(3), shape)
                    rc.mark(v.tensor_tensor(one[:], other, own, ALU.is_gt))
                    rc.link(v.tensor_tensor(two[:], other, own, ALU.is_equal))
                    rc.link(v.tensor_tensor(two[:], two[:], bcast(tri.unsqueeze(1), shape), ALU.mult))
                    rc.link(v.tensor_tensor(one[:], one[:], two[:], ALU.add))
                    rc.link(v.tensor_reduce(out[:], one[:], AX.X, ALU.add))

                rank(gs[:], NG, g1, g2, gr, C["tri_g"][:])
                rc.link(v.tensor_scalar(gr[:], gr[:], 1.5, None, ALU.is_lt))
                rc.link(v.tensor_scalar(pen[:], gr[:], 1.0, BIG, ALU.subtract, ALU.mult))
                s5 = sc[:].rearrange("p t (g e) -> p t g e", g=NG)
                rc.link(v.tensor_tensor(s5, s5, bcast(pen[:].unsqueeze(3), [P, GT, NG, EPG]), ALU.add))
                rank(sc[:], NE, e1, e2, er, C["tri_e"][:])
                v.scalar_tensor_tensor(out=comb[:, r, :, 0:NE], in0=er[:], scalar=1.5, in1=ex[:], op0=ALU.is_lt, op1=ALU.mult)\
                    .then_inc(comb_ready, 1)

            def gate(g, x):
                n = g * NX + x
                v.wait_ge(h3_ready, n + 1)
                v.wait_ge(silu_done, n + 1)
                wait_pos(v, y_ready, GT * (n - 1))
                v.scalar_tensor_tensor(out=hh[:, x % 2], in0=h3[x % 2][:], scalar=C["xb3"][:, x:x + 1], in1=si[:, x % 2],
                                       op0=ALU.add, op1=ALU.mult).then_inc(h_done, 1)

            def add(g, r, x):
                n = g * NX + x
                if x == 0:
                    wait_pos(v, out_ready, g)
                for t in range(GT):
                    if t % 2 == 0:
                        v.wait_ge(y_ready, GT * n + t + 2)
                    if x:
                        v.wait_ge(y_read, GT * (n - 1) + t + 1)
                    v.scalar_tensor_tensor(out=ya[:, t], in0=yp[t // 2][:, t % 2 * E:(t % 2 + 1) * E],
                                           scalar=comb[:, r, t, x:x + 1], in1=C["bs2"][:] if x == 0 else ya[:, t],
                                           op0=ALU.mult, op1=ALU.add).then_inc(y_read, 1)

            def body(g, i, r, left):
                v.wait_ge(comb_ready, g + 1)
                for x in range(NX):
                    gate(g, x)
                    if x:
                        add(g, r, x - 1)
                    if x in (4, 6):
                        n = (x - 4) // 2
                        v.wait_ge(be_ready, 2 * g + n + 1)
                        v.wait_ge(y_read, GT * (g * NX + x))
                        v.tensor_tensor(ya[:, 2 * n:2 * n + 2], ya[:, 2 * n:2 * n + 2],
                                        tp[1][:].rearrange("p (t e) -> p t e", t=2), ALU.add).then_inc(be_read, 1)
                        v.wait_ge(be_read, 2 * g + n + 1)
                    if x == 5 and left:
                        pre(g + 1, (r + 1) % 2, i + 1 + r, 1 + 2 * g)
                    if x == NEXT_AT + 1 and left:
                        shift(g + 1)
                    if x == NEXT_AT + 3 and left:
                        route(g + 1, (r + 1) % 2)
                add(g, r, NX - 1)
                v.wait_ge(y_read, GT * NX * (g + 1))
                ych.turn(g)
                mean_var(v, ych, C["go"], lambda t: ya[:, t], stats, mv, GT)
                power.ask(v, v.tensor_scalar(var[:], mv[:, :, 1], EPS, None, ALU.add), 1 + 2 * g + (1 if left else 0))
                for t in range(GT):
                    ych.mark(v.tensor_scalar(yb[:, t], ya[:, t], mv[:, t, 0:1], rstd[:, t:t + 1], ALU.subtract, ALU.mult))
                v.wait_ge(x_stored[r], 16 * (i + 1))
                ych.wait()
                v.tensor_tensor(xo[:, r], xs[:, r], yb[:], ALU.add).then_inc(out_ready, 1)

            pre(0, 0, 1, 0)
            shift(0)
            route(0, 0)
            turns(v, G, 2, body)


def program(nc, I, out):
    with ExitStack() as ctx:
        m = Mem(nc, ctx, "c")
        C = {
            "wqk": m.sb("wqk", [P, MATS, EC, E]), "wv": m.sb("wv", [P, EC, H * VD]),
            "w1t": m.sb("w1t", [P, EC, FF]), "w2t": m.sb("w2t", [P, FM, E]),
            "wo": m.sb("wo", [P, H * VD // P, E]), "b1": m.sb("b1", [P, FM]), "b2": m.sb("b2", [P, E]),
            "cw1": m.sb("cw1", [P, EC, 2 * E]), "cw2": m.sb("cw2", [P, EC, E]), "cb1": m.sb("cb1", [P, 2 * EC]),
            "cb2": m.sb("cb2", [P, E]), "filt": m.sb("filt", [P, EC, K]), "neglam": m.sb("neglam", [P, B * H]),
            "ident": m.sb("ident", [P, P]), "identb": m.sb("identb", [P, P], BF16), "mask": m.sb("mask", [P, P], BF16),
            "tri_g": m.sb("tri_g", [P, NG, NG]), "tri_e": m.sb("tri_e", [P, NE, NE]), "neghalf": m.sb("neghalf", [P, H * GT]),
            "s_qkv": m.sem("s_qkv"), "s_ffn": m.sem("s_ffn"), "s_conv": m.sem("s_conv"), "s_moe": m.sem("s_moe"), "go": m.sem("go"),
            "xw1": m.sb("xw1", [P, EC, NX, INTER]), "xw3": m.sb("xw3", [P, EC, NX, INTER]), "xw2": m.sb("xw2", [P, NX, E]),
            "xb1": m.sb("xb1", [P, NX]), "xb3": m.sb("xb3", [P, NX]), "xb2": m.sb("xb2", [NE, E]), "bs2": m.sb("bs2", [P, E]),
            "gw": m.sb("gw", [P, EC, NE]), "gb": m.sb("gb", [P, GT, NE]),
        }
        parts = nc.dram_tensor("parts", (3, MATS, B * E, S), BF16, kind="Internal").ap()
        values = nc.dram_tensor("values", (B * H, P, SB * VC), F32, kind="Internal").ap()
        heads = nc.dram_tensor("heads", (B * H, P, SB * VD), F32, kind="Internal").ap()
        prepare(nc, m, I, C)
        project(nc, I, C, I["x"], parts, values)
        attend(nc, I, C, parts, values, heads)
        x2 = nc.dram_tensor("x2", (B * S, E), F32, kind="Internal").ap()
        x3 = nc.dram_tensor("x3", (B * S, E), F32, kind="Internal").ap()
        merge_and_ffn(nc, I, C, heads, I["x"], x2)
        convolve(nc, I, C, x2, x3)
        experts(nc, I, C, x3, out)


def layouts(a):
    import numpy as np

    c = np.ascontiguousarray
    by = lambda v, n: c(v.reshape(n, P).T)
    return {
        "x": c(a["L0_attn_x"].reshape(B * S, E)),
        "wqk": np.stack([a["L0_attn_Wq1"], a["L0_attn_Wq2"], a["L0_attn_Wk1"], a["L0_attn_Wk2"]]),
        "Wv": a["L0_attn_Wv"], "Wo": a["L0_attn_Wo"],
        "lq1": a["L0_attn_lq1"], "lk1": a["L0_attn_lk1"], "lq2": a["L0_attn_lq2"], "lk2": a["L0_attn_lk2"],
        "w1t": c(a["L0_ffn_W1"].T), "b1": by(a["L0_ffn_b1"], FM), "w2t": c(a["L0_ffn_W2"].T), "b2": a["L0_ffn_b2"],
        "cw1": a["L1_attn_W1"], "cb1": by(a["L1_attn_b1"], 2 * EC), "cw2": a["L1_attn_W2"], "cb2": a["L1_attn_b2"],
        "cw": a["L1_attn_conv_shared_weight"],
        "gw": c(a["L1_ffn_gate_w"].T), "gb": a["L1_ffn_gate_b"],
        "We1": a["L1_ffn_We1"], "We2": a["L1_ffn_We2"], "We3": a["L1_ffn_We3"],
        "ws1": a["L1_ffn_ws1"], "ws2": a["L1_ffn_ws2"], "ws3": a["L1_ffn_ws3"],
        "xb1": np.concatenate([c(a["L1_ffn_be1"].T), by(a["L1_ffn_bs1"], NSH)], axis=1),
        "xb3": np.concatenate([c(a["L1_ffn_be3"].T), by(a["L1_ffn_bs3"], NSH)], axis=1),
        "be2": a["L1_ffn_be2"], "bs2": a["L1_ffn_bs2"],
    }


def kernel(**inputs):
    import numpy as np
    import concourse.bacc as bacc
    from concourse.bass_utils import run_bass_kernel_spmd

    nc = bacc.Bacc("TRN2", target_bir_lowering=False, num_devices=1)
    arrays, aps = {}, {}
    for name, a in layouts({k: np.asarray(v) for k, v in inputs.items()}).items():
        arrays[f"in_{name}"] = np.ascontiguousarray(a)
        aps[name] = nc.dram_tensor(f"in_{name}", a.shape, mybir.dt.from_np(a.dtype), kind="ExternalInput").ap()
    out = nc.dram_tensor("out_x", (B * S, E), F32, kind="ExternalOutput").ap()
    program(nc, aps, out)
    r = run_bass_kernel_spmd(nc, [arrays], core_ids=[0])
    return r.results[0]["out_x"].reshape(B, S, E)
```

```python
import math
from contextlib import ExitStack

import concourse.bass as bass
from concourse import mybir

F32, BF16 = mybir.dt.float32, mybir.dt.bfloat16
ALU, ACT, AX = mybir.AluOpType, mybir.ActivationFunctionType, mybir.AxisListType

P = 128
B, S, E = 8, 1024, 256
H, D = 16, 16
VD = 2 * D
VC = VD
VO = VD + 1
EC = E // P
GT = 4
GN = GT * P
G = B * S // GN
GB = S // GN
SB = S // P
MATS = 4
FF = 4 * E
FM = FF // P
K = 15
PAD = K // 2
NE, NG, INTER, NSH = 16, 4, 128, 2
NX = NE + NSH
EPG = NE // NG
EPS = 1e-5
LAM_INIT = 0.8 - 0.6 * math.exp(-0.3 * (12 - 1))
MASKED = -1e30
BIG = 1e30


class Chain:

    def __init__(self, eng, sem, per_turn=0):
        self.eng, self.sem, self.per, self.base, self.n = eng, sem, per_turn, 0, 0

    def turn(self, g):
        assert self.n in (0, self.per), (self.n, self.per)
        self.base, self.n = g * self.per, 0

    def mark(self, ins):
        ins.then_inc(self.sem, 1)
        self.n += 1

    def wait(self):
        self.eng.wait_ge(self.sem, self.base + self.n)

    def link(self, ins):
        self.mark(ins)
        self.wait()


def at(ap, g):
    one = ap[g:g + 1] if isinstance(g, int) else ap[bass.ds(g, 1)]
    names = [f"d{n}" for n in range(len(ap.shape) - 1)]
    return one.rearrange(f"a {' '.join(names)} -> (a {names[0]}) {' '.join(names[1:])}")


def turns(eng, n, unroll, body):
    for r in range(unroll):
        body(r, 0, r, unroll)
    with eng.Fori(1, n // unroll - 1) as i:
        for r in range(unroll):
            body(i * unroll + r, i, r, unroll)
    i = n // unroll - 1
    for r in range(unroll):
        body(i * unroll + r, i, r, unroll - 1 - r)


def wait_pos(eng, sem, value):
    if not isinstance(value, int) or value > 0:
        eng.wait_ge(sem, value)


def wait_apart(eng, go, sem, value):
    if isinstance(value, int):
        eng.wait_ge(sem, value)
        return
    with eng.register() as count:
        eng.reg_mov(count, value)
        eng.wait_ge(go, 1)
        eng.wait_ge(sem, count)


class Mem:

    def __init__(self, nc, ctx, tag):
        self.nc, self.ctx, self.tag = nc, ctx, tag

    def sb(self, name, shape, dt=F32):
        return self.ctx.enter_context(self.nc.sbuf_tensor(f"{self.tag}_{name}", shape, dt))

    def ps(self, name, shape=(P, 512)):
        return self.ctx.enter_context(self.nc.psum_tensor(f"{self.tag}_{name}", list(shape), F32))

    def sem(self, name):
        return self.nc.semaphore(f"{self.tag}_{name}").__enter__()

    def sems(self, name, n):
        return [self.sem(f"{name}{i}") for i in range(n)]


def mean_var(v, chain, go, src, stats, mv, tiles):
    for t in range(tiles):
        chain.mark(v.bn_stats(stats[:, t, :], src(t)))
    wait_apart(v, go, chain.sem, chain.base + chain.n)
    for t in range(tiles):
        chain.mark(v.bn_aggr(mv[:, t, :], stats[:, t, :]))
    chain.wait()


def bcast(ap, shape):
    return ap.to_broadcast(shape)


def prepare(nc, I, C):
    with ExitStack() as ctx:
        t = Mem(nc, ctx, "pre")
        wload, small = t.sem("wload"), t.sem("small")
        zeroed, poolc, vec, acts, tot = (t.sem(n) for n in ("zeroed", "poolc", "vec", "acts", "tot"))
        ones = t.sb("ones", [P, P])
        part = t.sb("part", [P, 2])
        thr = C["thr"]
        lqk = t.sb("lqk", [P, 4, H * D])
        lsum = t.sb("lsum", [P, 2, H])
        fmax = t.sb("fmax", [P, EC])
        wmean = t.sb("wmean", [P, EC * H])
        centre = t.sem("centre")
        fsum = t.sb("fsum", [P, EC])
        psum = t.ps("tot")
        block = ctx.enter_context(nc.Block())

        @block.sync
        def _(sp):
            sp.dma_start(C["wqk"][:], I["wqk"].rearrange("m (c p) n -> p m c n", p=P)).then_inc(C["s_qkv"], 16)
            sp.dma_start(C["wv"][:], I["Wv"].rearrange("(c p) n -> p c n", p=P)).then_inc(C["s_qkv"], 16)
            sp.dma_start(C["w1t"][:], I["w1t"].rearrange("(c p) n -> p c n", p=P)).then_inc(wload, 16)
            sp.dma_start(C["w2t"][:], I["w2t"].rearrange("(c p) n -> p c n", p=P)).then_inc(wload, 16)
            for h in range(H):
                r = h * D % P
                sp.dma_start(C["filt"][r:r + D, h * D // P, :],
                             I["cw"][h, :].partition_broadcast(D)).then_inc(small, 16)
            for n, name in enumerate(("lq1", "lk1", "lq2", "lk2")):
                sp.dma_start(lqk[:, n, :], I[name].rearrange("h d -> (h d)").partition_broadcast(P)).then_inc(small, 16)
            sp.dma_start(C["fold"][:], I["fold"]).then_inc(small, 16)

        @block.gpsimd
        def _(pool):
            pool.memset(C["ident"][:], 0.0).then_inc(zeroed, 1)
            pool.memset(C["mask"][:], 0.0).then_inc(zeroed, 1)
            pool.memset(C["identb"][:], 0.0).then_inc(zeroed, 1)
            pool.memset(C["tri_g"][:], 1.0).then_inc(zeroed, 1)
            pool.memset(C["tri_e"][:], 1.0).then_inc(zeroed, 1)
            pool.memset(C["neghalf"][:], -0.5).then_inc(zeroed, 1)
            pool.wait_ge(zeroed, 6)
            for x in ("ident", "identb"):
                pool.affine_select(out=C[x][:], in_=C[x][:], compare_op=ALU.not_equal, fill=1.0, base=0,
                                   pattern=[[-1, P]], channel_multiplier=1).then_inc(poolc, 1)
            pool.affine_select(out=C["mask"][:], in_=C["mask"][:], compare_op=ALU.is_ge, fill=MASKED, base=0,
                               pattern=[[-1, P]], channel_multiplier=1).then_inc(poolc, 1)
            pool.affine_select(out=C["tri_g"][:], in_=C["tri_g"][:], compare_op=ALU.is_gt, fill=0.0, base=0,
                               pattern=[[1, NG], [-1, NG]], channel_multiplier=0).then_inc(poolc, 1)
            pool.affine_select(out=C["tri_e"][:], in_=C["tri_e"][:], compare_op=ALU.is_gt, fill=0.0, base=0,
                               pattern=[[1, NE], [-1, NE]], channel_multiplier=0).then_inc(poolc, 1)
            pool.wait_ge(poolc, 5)

        @block.tensor
        def _(pe):
            pe.wait_ge(vec, 3)
            nc.tensor.matmul(psum[:, 0:2], ones[:], part[:], start=True, stop=True).then_inc(tot, 1)

        @block.scalar
        def _(act):
            act.wait_ge(vec, 9)
            nc.scalar.activation(lsum[:], lsum[:], ACT.Exp).then_inc(acts, 1)
            for c in range(EC):
                nc.scalar.activation(C["filt"][:, c, :], C["filt"][:, c, :], ACT.Exp).then_inc(acts, 1)

        @block.vector
        def _(v):
            ch = Chain(v, vec)
            v.sem_inc(C["go"], 1)
            ch.mark(v.memset(ones[:], 1.0))
            v.wait_ge(C["s_qkv"], 32)
            wv = C["wv"][:].rearrange("p c (h v) -> p (c h) v", h=H)
            v.tensor_reduce(wmean[:], wv, AX.X, ALU.add).then_inc(centre, 1)
            v.wait_ge(centre, 1)
            v.tensor_scalar(wmean[:], wmean[:], 1.0 / VD, None, ALU.mult).then_inc(centre, 1)
            v.wait_ge(centre, 2)
            v.tensor_tensor(wv, wv, bcast(wmean[:].unsqueeze(2), [P, EC * H, VD]), ALU.subtract).then_inc(centre, 1)
            v.wait_ge(wload, 32)
            w = [C["w1t"][:].rearrange("p c n -> p (c n)"), C["w2t"][:].rearrange("p c n -> p (c n)")]
            for n in range(2):
                ch.mark(v.tensor_reduce(part[:, n:n + 1], w[n], AX.X, ALU.add, apply_absolute_value=True))
            assert ch.n == 3
            v.wait_ge(small, 16 * (H + 5))
            for n in range(2):
                ch.link(v.tensor_tensor(lqk[:, 2 * n, :], lqk[:, 2 * n, :], lqk[:, 2 * n + 1, :], ALU.mult))
                ch.mark(v.tensor_reduce(lsum[:, n, :], lqk[:, 2 * n, :].rearrange("p (h d) -> p h d", h=H), AX.X, ALU.add))
            ch.link(v.tensor_reduce(fmax[:], C["filt"][:], AX.X, ALU.max))
            assert ch.n == 8
            v.tensor_tensor(C["filt"][:], C["filt"][:], bcast(fmax[:].unsqueeze(2), [P, EC, K]), ALU.subtract).then_inc(vec, 1)
            ch.n += 1
            v.wait_ge(acts, 1 + EC)
            ch.link(v.tensor_tensor(lsum[:, 0, :], lsum[:, 1, :], lsum[:, 0, :], ALU.subtract))
            for b in range(B):
                ch.mark(v.tensor_scalar(C["neglam"][:, b * H:(b + 1) * H], lsum[:, 0, :], -LAM_INIT, None, ALU.add))
            ch.link(v.tensor_reduce(fsum[:], C["filt"][:], AX.X, ALU.add))
            ch.link(v.reciprocal(fsum[:], fsum[:]))
            ch.link(v.tensor_tensor(C["filt"][:], C["filt"][:], bcast(fsum[:].unsqueeze(2), [P, EC, K]), ALU.mult))
            v.wait_ge(tot, 1)
            ch.link(v.tensor_scalar(thr[:, :, 0], psum[:, 0:2], 1.0 / (FF * E), 1e-8, ALU.mult, ALU.max))
            ch.link(v.tensor_scalar(thr[:, :, 1], thr[:, :, 0], -0.5, None, ALU.mult))
            ch.link(v.tensor_scalar(thr[:, :, 0], thr[:, :, 0], 0.5, None, ALU.mult))


def later_weights(I, C):
    w = []
    for name, we, ws in (("xw1", "We1", "ws1"), ("xw3", "We3", "ws3")):
        for c in range(EC):
            w.append((C[name][:, c, 0:NE], I[we].rearrange("e (c p) n -> c p e n", p=P)[c], C["s_moe"]))
            w.append((C[name][:, c, NE:NX], I[ws].rearrange("(c p) (x n) -> c p x n", p=P, x=NSH)[c], C["s_moe"]))
    w += [(C["xw2"][:, 0:NE], I["We2"].rearrange("e p n -> p e n"), C["s_moe"]),
          (C["xw2"][:, NE:NX], I["ws2"].rearrange("(x p) n -> p x n", p=P), C["s_moe"]),
          (C["xb1"][:], I["xb1"], C["s_moe"]), (C["xb3"][:], I["xb3"], C["s_moe"]), (C["xb2"][:], I["be2"], C["s_moe"]),
          (C["bs2"][:], I["bs2"].partition_broadcast(P), C["s_moe"]),
          (C["gw"][:], I["gw"].rearrange("(c p) e -> p c e", p=P), C["s_moe"])]
    w += [(C["gb"][:, t], I["gb"].partition_broadcast(P), C["s_moe"]) for t in range(GT)]
    C["n_moe"] = 16 * len(w)
    w += [(C["wo"][:], I["Wo"].rearrange("(c p) n -> p c n", p=P), C["s_ffn"]), (C["b1"][:], I["b1"], C["s_ffn"]),
          (C["b2"][:], I["b2"].partition_broadcast(P), C["s_ffn"]),
          (C["cw1"][:], I["cw1"].rearrange("(c p) n -> p c n", p=P), C["s_conv"]),
          (C["cw2"][:], I["cw2"].rearrange("(c p) n -> p c n", p=P), C["s_conv"]),
          (C["cb1"][:], I["cb1"], C["s_conv"]), (C["cb2"][:], I["cb2"].partition_broadcast(P), C["s_conv"])]
    return w


def project(nc, I, C, x_in, parts, values):
    with ExitStack() as ctx:
        m = Mem(nc, ctx, "prj")
        x = m.sb("x", [P, 2, GT, E])
        xn = m.sb("xn", [P, GT, E])
        xt = m.sb("xt", [P, 2, EC, GN])
        stats, mv, var, rstd = m.sb("stats", [P, GT, 6]), m.sb("mv", [P, GT, 2]), m.sb("var", [P, GT]), m.sb("rstd", [P, GT])
        pt = m.sb("pt", [P, 4, 3, GN], BF16)
        rest = m.sb("rest", [P, 2, GN])
        vs = m.sb("vs", [P, 2, H, GT, VC])
        tp = [m.ps(f"tp{i}") for i in range(2)]
        qk = [m.ps(f"qk{i}") for i in range(4)]
        vp = [m.ps(f"v{i}") for i in range(2)]
        x_loaded, part_stored, v_stored = m.sems("x_loaded", 2), m.sems("part_stored", 4), m.sems("v_stored", 2)
        (stat, var_ready, rstd_ready, xn_ready, tp_ready, xt_ready, qk_ready, qk_split, hi_ready, split, parts_ready,
         v_ready, v_copied, ones_set) = (m.sem(n) for n in (
             "stat", "var_ready", "rstd_ready", "xn_ready", "tp_ready", "xt_ready", "qk_ready", "qk_split", "hi_ready",
             "split", "parts_ready", "v_ready", "v_copied", "ones_set"))
        NQ = MATS * EC
        xg = x_in.rearrange("(g t p) e -> g p t e", p=P, t=GT)
        pg = parts.rearrange("k m (b c p) (h n) -> b h m c p k n", b=B, c=EC, h=GB)
        vg = values.rearrange("(b h) p (c t v) -> b c p h (t v)", b=B, c=GB, t=GT)
        block = ctx.enter_context(nc.Block())

        @block.sync
        def _(sp):
            for g in range(2):
                sp.dma_start(x[:, g], at(xg, g)).then_inc(x_loaded[g], 16)

            def body(g, i, r, left):
                if left >= 2:
                    sp.wait_ge(xn_ready, g + 1)
                    sp.dma_start(x[:, r], at(xg, g + 2)).then_inc(x_loaded[r], 16)
                for n in range(NQ):
                    sp.wait_ge(parts_ready, g * NQ + n + 1)
                    sp.dma_start(part_dst(i, r, n), pt[:, n % 4]).then_inc(part_stored[n % 4], 16)
                sp.wait_ge(v_copied, g * GT + GT + 2)
                sp.dma_start(value_dst(i, r), vs[:, r].rearrange("p h t v -> p h (t v)")).then_inc(v_stored[r], 16)

            def part_dst(i, r, n):
                return at(pg[:, r, n // EC, n % EC], i)

            def value_dst(i, r):
                return at(vg[:, r], i)

            turns(sp, G, GB, body)
            for n in range(4):
                sp.wait_ge(part_stored[n], 16 * (G * NQ // 4 + 1))
            for r in range(2):
                sp.wait_ge(v_stored[r], 16 * (G // 2 + 1))

        @block.gpsimd
        def _(pool):
            pool.memset(vs[:, :, :, :, VC - 1:VC].rearrange("p s h t o -> p (s h t) o"), 1.0).then_inc(ones_set, 1)

            def rstd_of(g):
                pool.wait_ge(var_ready, g + 1)
                nc.gpsimd.tensor_tensor(rstd[:], var[:], C["neghalf"][:, 0:GT], ALU.pow).then_inc(rstd_ready, 1)

            rstd_of(0)
            turns(pool, G, 2, lambda g, i, r, left: rstd_of(g + 1) if left else None)

        @block.vector
        def _(v):
            st = Chain(v, stat, 2 * GT)
            sp_ = Chain(v, split, NQ)
            v.sem_inc(qk_split, 4)

            def pre(g, r, uses):
                st.turn(g)
                v.wait_ge(x_loaded[r], 16 * uses)
                mean_var(v, st, C["go"], lambda t: x[:, r, t], stats, mv, GT)
                v.tensor_scalar(var[:], mv[:, :, 1], EPS, None, ALU.add).then_inc(var_ready, 1)
                v.wait_ge(rstd_ready, g + 1)
                for t in range(GT):
                    ins = v.tensor_scalar(xn[:, t], x[:, r, t], mv[:, t, 0:1], rstd[:, t:t + 1], ALU.subtract, ALU.mult)
                ins.then_inc(xn_ready, 1)

            def body(g, i, r, left):
                sp_.turn(g)
                for n in range(NQ):
                    if n == 4 and left:
                        pre(g + 1, (r + 1) % 2, i + 1 + r)
                    v.wait_ge(hi_ready, g * NQ + n + 1)
                    v.tensor_tensor(rest[:, n % 2], qk[n % 4][:], pt[:, n % 4, 0], ALU.subtract).then_inc(qk_split, 1)
                    v.wait_ge(qk_split, g * NQ + n + 1 + 4)
                    sp_.link(v.tensor_copy(pt[:, n % 4, 1], rest[:, n % 2]))
                    v.tensor_tensor(pt[:, n % 4, 2], rest[:, n % 2], pt[:, n % 4, 1], ALU.subtract).then_inc(parts_ready, 1)

            pre(0, 0, 1)
            turns(v, G, 2, body)

        @block.scalar
        def _(act):
            for n in range(4):
                act.sem_inc(part_stored[n], 16)
            for r in range(2):
                act.sem_inc(v_stored[r], 16)
            act.sem_inc(v_copied, 2)
            act.wait_ge(ones_set, 1)

            def xt_copy(g, r):
                for c in range(EC):
                    act.wait_ge(tp_ready, g * EC + c + 1)
                    act.activation(xt[:, r, c], tp[c][:], ACT.Copy).then_inc(xt_ready, 1)

            def body(g, i, r, left):
                for n in range(NQ):
                    act.wait_ge(qk_ready, g * NQ + n + 1)
                    act.wait_ge(part_stored[n % 4], 16 * (g * (NQ // 4) + n // 4 + 1))
                    act.activation(pt[:, n % 4, 0], qk[n % 4][:], ACT.Copy).then_inc(hi_ready, 1)
                if left:
                    xt_copy(g + 1, (r + 1) % 2)
                act.wait_ge(v_stored[r], 16 * (i + 1))
                for t in range(GT):
                    act.wait_ge(v_ready, g * GT + t + 1)
                    act.activation(vs[:, r, :, t, 0:VC - 1], vp[t % 2][:].rearrange("p (h v) -> p h v", h=H)[:, :, 0:VC - 1],
                                   ACT.Copy).then_inc(v_copied, 1)

            xt_copy(0, 0)
            turns(act, G, 2, body)

        @block.tensor
        def _(pe):
            pe.wait_ge(C["s_qkv"], 32)

            def transposes(g):
                pe.wait_ge(xn_ready, g + 1)
                for c in range(EC):
                    for t in range(GT):
                        ins = nc.tensor.transpose(tp[c][:, t * P:(t + 1) * P], xn[:, t, c * P:(c + 1) * P], C["ident"][:])
                    ins.then_inc(tp_ready, 1)

            def body(g, i, r, left):
                pe.wait_ge(xt_ready, (g + 1) * EC)
                for n in range(NQ):
                    pe.wait_ge(qk_split, g * NQ + n + 1)
                    for c in range(EC):
                        ins = nc.tensor.matmul(qk[n % 4][:], C["wqk"][:, n // EC, c, n % EC * P:(n % EC + 1) * P],
                                               xt[:, r, c], start=(c == 0), stop=(c == EC - 1))
                    ins.then_inc(qk_ready, 1)
                if left:
                    transposes(g + 1)
                for t in range(GT):
                    pe.wait_ge(v_copied, g * GT + t + 1)
                    for c in range(EC):
                        ins = nc.tensor.matmul(vp[t % 2][:], xt[:, r, c, t * P:(t + 1) * P], C["wv"][:, c],
                                               start=(c == 0), stop=(c == EC - 1))
                    ins.then_inc(v_ready, 1)

            transposes(0)
            turns(pe, G, 2, body)


def attend(nc, I, C, parts, values, heads):
    PAIRS = [(0, 0), (0, 1), (1, 0), (1, 1), (0, 2), (2, 0)]
    KR = len(PAIRS) * D
    SL = 4
    T = B * H
    HB = GN // P
    SCALE = 1.0 / math.sqrt(D)
    OW = 2 * VO
    ST = [(half, j, mp, max(0, j - HB * half) * P) for half in (1, 0) for j in range(HB * (half + 1)) for mp in range(2)]
    NST = len(ST)
    at_st = {(half, j): n for n, (half, j, mp, off) in enumerate(ST) if mp}
    NSEL = 2 * 2 * HB
    ITEMS = [(mp, i) for mp in range(2) for k in range(HB) for i in (HB + k, k)]
    NI = len(ITEMS)
    ITEM_AT = [0, 1, 3, 4, 6, 8, 9, 10, 11, 12, 13, 15, 17, 18, 20, 23]
    LAG = 5
    PV1_AT = {min(at_st[1, j] + LAG - 1, NST - 1): j for j in range(1, SB, 2)}
    PV0_AT = {1 + j: j for j in range(1, HB, 2)}
    ROWS_AT = 1
    END1_AT = 3
    END0_AT = 12
    with ExitStack() as ctx:
        m = Mem(nc, ctx, "att")
        ops = m.sb("ops", [KR + 3, SL, MATS, S], BF16)
        va = m.sb("va", [P, SL, SB, VC])
        pr = [m.sb("p0", [P, 2, HB, GN]), m.sb("p1", [P, 2, SB, GN])]
        mcol = m.sb("mcol", [P, 2 * SB])
        mneg = m.sb("mneg", [2 * SB, 2, P])
        mpart = m.sb("mpart", [2 * SB, 3, P], BF16)
        ot = [m.sb("ot0", [P, GN]), m.sb("ot1", [P, GN])]
        rl = m.sb("rl", [P, HB, 2])
        o12 = m.sb("o12", [P, 2, HB, VD])
        ofin = m.sb("ofin", [P, 2, SB, VD])
        smax = [m.ps("smax_s"), m.ps("smax_b", (P, 1024))]
        tp = m.ps("tp")
        stp = [m.ps(f"st{i}") for i in range(2)]
        op = [m.ps(f"pv{i}") for i in range(2)]
        loaded, max_placed, o_stored = m.sems("loaded", SL), m.sems("max_placed", SL), m.sems("o_stored", 2)
        pv_done, o_copied = m.sems("pv_done", 2), m.sems("o_copied", 2)
        (ones_set, sm_ready, sm_reduced, mt_ready, mp_steps, mt_read, mp_ready, st_ready, exp_done, masked,
         ot_ready, ot_read, norm_steps, head_ready, rows_set) = (m.sem(n) for n in (
             "ones_set", "sm_ready", "sm_reduced", "mt_ready", "mp_steps", "mt_read", "mp_ready", "st_ready", "exp_done",
             "masked", "ot_ready", "ot_read", "norm_steps", "head_ready", "rows_set"))
        pd = parts.rearrange("k m (t d) n -> t k m d n", d=D)
        LOADS = 16 * (2 * len(PAIRS) + 1)
        PLACED = 16 * 3

        block = ctx.enter_context(nc.Block())

        @block.sync
        def _(sp):
            def load(t, s):
                for n, (a, b) in enumerate(PAIRS):
                    for side, part in ((0, a), (2, b)):
                        one = pd[t:t + 1, part, side:side + 2] if isinstance(t, int) else pd[bass.ds(t, 1), part, side:side + 2]
                        sp.dma_start(ops[n * D:(n + 1) * D, s, side:side + 2, :],
                                     one.rearrange("a m d n -> (a d) m n")).then_inc(loaded[s], 16)
                sp.dma_start(va[:, s].rearrange("p t v -> p (t v)"), at(values, t)).then_inc(loaded[s], 16)

            def place(t, s):
                sp.wait_ge(mp_ready, t + 1)
                for k in range(3):
                    sp.dma_start(ops[KR + k:KR + k + 1, s, 0:2, :], mpart[:, k, :]).then_inc(max_placed[s], 16)

            def store(t, q):
                sp.wait_ge(head_ready, 2 * (t + 1))
                sp.dma_start(at(heads, t), ofin[:, q].rearrange("p b v -> p (b v)")).then_inc(o_stored[q], 16)

            def body(t, i, r, left):
                if left >= 1:
                    place(t + 1, (r + 1) % SL)
                if left >= 3:
                    wait_pos(sp, pv_done[0], t)
                    load(t + 3, (r + 3) % SL)
                if not isinstance(t, int) or t:
                    store(t - 1, (r - 1) % 2)
                if isinstance(t, int) and t < SL:
                    for dst, src, sem in later[t::SL]:
                        sp.dma_start(dst, src).then_inc(sem, 16)

            later = later_weights(I, C)
            for t in range(3):
                load(t, t)
            sp.wait_ge(ones_set, 1)
            place(0, 0)
            turns(sp, T, SL, body)
            store(T - 1, (T - 1) % 2)
            for r in range(2):
                sp.wait_ge(o_stored[r], 16 * (T // 2))

        @block.tensor
        def _(pe):
            def max_item(t, s, n):
                mp, i = ITEMS[n]
                wait_pos(pe, sm_reduced, t * NI + n - 1)
                out, w = smax[i >= HB], (i + 1) * P
                for c in range(0, w, GN):
                    k = min(GN, w - c)
                    nc.tensor.matmul(out[:, c:c + k], ops[0:KR, s, mp, i * P:w], ops[0:KR, s, 2 + mp, c:c + k],
                                     start=True, stop=(c + k < w))
                nc.tensor.matmul(out[:, i * P:w], C["identb"][:], C["mask"][:], start=False, stop=True)\
                    .then_inc(sm_ready, 1)

            def max_rows(t):
                pe.wait_ge(sm_reduced, (t + 1) * NI)
                nc.tensor.transpose(tp[0:2 * SB, 0:P], mcol[:], C["ident"][:]).then_inc(mt_ready, 1)

            def scores(t, s, n):
                half, j, mp, off = ST[n]
                wait_pos(pe, exp_done, t * NST + n - 1)
                nc.tensor.matmul(stp[n % 2][:, off:GN], ops[:, s, 2 + mp, j * P:(j + 1) * P],
                                 ops[:, s, mp, half * GN + off:(half + 1) * GN], start=True, stop=True).then_inc(st_ready, 1)

            def pv(t, s, half, j):
                last = HB * (half + 1) - 1
                if j == 1:
                    wait_pos(pe, o_copied[half], t)
                pe.wait_ge(exp_done, t * NST + at_st[half, j] + 1)
                if j >= HB * half:
                    pe.wait_ge(masked, t * NSEL + (1 - half) * 2 * HB + 2 * (j - HB * half + 1))
                for odd in range(2):
                    k = j - 1 + odd
                    off = max(0, k - HB * half) * P if k > 1 else 0
                    for mp in range(2):
                        row = (2 * odd + mp) * VC
                        ins = nc.tensor.matmul(op[half][row:row + VC, off:GN], va[:, s, k, :], pr[half][:, mp, k, off:GN],
                                               start=(j == 1), stop=(j == last), tile_position=(0, row))
                if j == last:
                    ins.then_inc(pv_done[half], 1)

            def end(t, half, mt):
                pe.wait_ge(o_copied[half], t + 1)
                wait_pos(pe, ot_read, 2 * t + (1 - half))
                if mt:
                    pe.wait_ge(mt_read, t + 3)
                for b in range(HB):
                    ins = nc.tensor.matmul(tp[:, b * OW:(b + 1) * OW], ot[half][:, b * P:(b + 1) * P], C["fold"][:],
                                           start=True, stop=True)
                ins.then_inc(ot_ready, 1)

            def body(t, i, r, left):
                s, s1, s2 = r, (r - 1) % SL, (r + 2) % SL
                first = isinstance(t, int) and t == 0
                pe.wait_ge(max_placed[s], PLACED * (i + 1))
                if left >= 2:
                    pe.wait_ge(loaded[s2], LOADS * (i + 1 + (r >= 2)))
                for n in range(NST):
                    scores(t, s, n)
                    if n == ROWS_AT and left >= 1:
                        wait_pos(pe, ot_read, 2 * (t - 1))
                        max_rows(t + 1)
                    if not first and n == END1_AT:
                        end(t - 1, 1, left >= 1)
                    if not first and n in PV0_AT:
                        pv(t - 1, s1, 0, PV0_AT[n])
                    if not first and n == END0_AT:
                        end(t - 1, 0, False)
                    if n in PV1_AT:
                        pv(t, s, 1, PV1_AT[n])
                    if left >= 2:
                        for k in range(NI):
                            if ITEM_AT[k] == n:
                                max_item(t + 2, s2, k)

            pe.wait_ge(rows_set, 1)
            pe.wait_ge(loaded[0], LOADS)
            for n in range(NI):
                max_item(0, 0, n)
            max_rows(0)
            pe.wait_ge(loaded[1], LOADS)
            pe.wait_ge(mt_read, 1)
            for n in range(NI):
                max_item(1, 1, n)
            turns(pe, T, SL, body)
            end(T - 1, 1, False)
            for j in range(1, HB, 2):
                pv(T - 1, (T - 1) % SL, 0, j)
            end(T - 1, 0, False)

        @block.scalar
        def _(act):
            def copy_o(t, half):
                act.wait_ge(pv_done[half], t + 1)
                wait_pos(act, ot_ready, 2 * t - half)
                act.activation(ot[half][:], op[half][:], ACT.Copy).then_inc(o_copied[half], 1)

            def body(t, i, r, left):
                for n, (half, j, mp, off) in enumerate(ST):
                    if j == 0 and mp == 0:
                        wait_pos(act, pv_done[half], t)
                    act.wait_ge(st_ready, t * NST + n + 1)
                    act.activation(pr[half][:, mp, j, off:GN], stp[n % 2][:, off:GN], ACT.Exp, scale=SCALE).then_inc(exp_done, 1)
                    if n == COPY0_AT and not (isinstance(t, int) and t == 0):
                        copy_o(t - 1, 0)
                copy_o(t, 1)

            COPY0_AT = 9
            turns(act, T, SL, body)
            copy_o(T - 1, 0)

        @block.gpsimd
        def _(pool):
            pool.memset(ops[KR:KR + 3, :, :, :].rearrange("p s m n -> p (s m n)"), 1.0).then_inc(ones_set, 1)

            def body(t, i, r, left):
                for n, (half, j, mp, off) in enumerate(ST):
                    if j >= HB * half:
                        wait_apart(pool, ones_set, exp_done, t * NST + n + 1)
                        d = pr[half][:, mp, j, off:off + P]
                        pool.affine_select(out=d, in_=d, compare_op=ALU.is_ge, fill=0.0, base=0,
                                           pattern=[[1, P]], channel_multiplier=-1).then_inc(masked, 1)

            turns(pool, T, SL, body)

        @block.vector
        def _(v):
            v.memset(pr[0][:, :, 1, 0:P], 0.0).then_inc(rows_set, 1)
            mc = Chain(v, mp_steps, 3)
            nch = Chain(v, norm_steps, 3)

            def reduce_item(t, n):
                mp, i = ITEMS[n]
                v.wait_ge(sm_ready, t * NI + n + 1)
                v.tensor_reduce(mcol[:, mp * SB + i:mp * SB + i + 1], smax[i >= HB][:, 0:(i + 1) * P], AX.X, ALU.max)\
                    .then_inc(sm_reduced, 1)

            def max_parts(t, s, uses):
                mc.turn(t)
                v.wait_ge(mt_ready, t + 1)
                v.tensor_scalar(mneg[:, 0], tp[0:2 * SB, 0:P], -1.0, None, ALU.mult).then_inc(mt_read, 1)
                v.wait_ge(mt_read, t + 1)
                if not isinstance(uses, int) or uses:
                    v.wait_ge(max_placed[s], PLACED * uses)
                mc.link(v.tensor_copy(mpart[:, 0], mneg[:, 0]))
                mc.link(v.tensor_tensor(mneg[:, 1], mneg[:, 0], mpart[:, 0], ALU.subtract))
                mc.link(v.tensor_copy(mpart[:, 1], mneg[:, 1]))
                v.tensor_tensor(mpart[:, 2], mneg[:, 1], mpart[:, 1], ALU.subtract).then_inc(mp_ready, 1)

            def norm(t, q, uses, half):
                k = 2 * t + (1 - half)
                nch.turn(k)
                v.wait_ge(ot_ready, k + 1)
                o = tp[:, 0:HB * OW].rearrange("p (b w) -> p b w", b=HB)
                nch.link(v.reciprocal(rl[:], o[:, :, VD:OW:VO]))
                lam = C["neglam"][:, t:t + 1] if isinstance(t, int) else C["neglam"][:, bass.ds(t, 1)]
                nch.mark(v.tensor_tensor(o12[:, 0], o[:, :, 0:VD], bcast(rl[:, :, 0:1], [P, HB, VD]), ALU.mult))
                nch.link(v.tensor_scalar(rl[:, :, 1], rl[:, :, 1], lam, None, ALU.mult))
                v.tensor_tensor(o12[:, 1], o[:, :, VO:VO + VD], bcast(rl[:, :, 1:2], [P, HB, VD]), ALU.mult).then_inc(ot_read, 1)
                v.wait_ge(ot_read, k + 1)
                wait_pos(v, o_stored[q], 16 * uses)
                v.tensor_tensor(ofin[:, q, half * HB:(half + 1) * HB], o12[:, 0], o12[:, 1], ALU.add).then_inc(head_ready, 1)

            def body(t, i, r, left):
                if left >= 1:
                    max_parts(t + 1, r, i + 1)
                for n in range(NI):
                    if left >= 2:
                        reduce_item(t + 2, n)
                    if n in NORM_AT and not (isinstance(t, int) and t == 0):
                        norm(t - 1, (r - 1) % 2, 2 * i + (r - 1) // 2, NORM_AT[n])

            NORM_AT = {3: 1, 10: 0}
            for n in range(NI):
                reduce_item(0, n)
            max_parts(0, 0, 0)
            for n in range(NI):
                reduce_item(1, n)
            turns(v, T, SL, body)
            for half in (1, 0):
                norm(T - 1, (T - 1) % 2, (T - 1) // 2, half)


class Power:

    def __init__(self, m, C):
        self.asked, self.told, self.C = m.sem("var_ready"), m.sem("rstd_ready"), C

    def request(self, ins):
        ins.then_inc(self.asked, 1)

    def receive(self, v, k):
        v.wait_ge(self.told, k + 1)

    def ask(self, v, ins, k):
        self.request(ins)
        self.receive(v, k)

    def serve(self, nc, pool, var, rstd, k):
        pool.wait_ge(self.asked, k + 1)
        nc.gpsimd.tensor_tensor(rstd, var, self.C["neghalf"][:, 0:var.shape[1]], ALU.pow).then_inc(self.told, 1)


def merge_and_ffn(nc, I, C, heads, x_in, x_out):
    HC = H * VD // P
    with ExitStack() as ctx:
        m = Mem(nc, ctx, "ffn")
        os_ = m.sb("os", [P, 2, H, GT, VD])
        xs = m.sb("xs", [P, 2, GT, E])
        xc, sq = m.sb("xc", [P, H * GT, VD]), m.sb("sq", [P, H * GT, VD])
        hm, hv, hr = m.sb("hm", [P, H * GT]), m.sb("hv", [P, H * GT]), m.sb("hr", [P, H * GT])
        on, mt = m.sb("on", [P, GT, H * VD]), m.sb("mt", [P, HC, GN])
        x1, xn, xt = m.sb("x1", [P, 2, GT, E]), m.sb("xn", [P, GT, E]), m.sb("xt", [P, EC, GN])
        ht = m.sb("ht", [P, FM, GN])
        yb, yn, xo = m.sb("yb", [P, GT, E]), m.sb("yn", [P, GT, E]), m.sb("xo", [P, 2, GT, E])
        stats, mv = m.sb("stats", [P, GT, 6]), m.sb("mv", [P, GT, 2])
        var, rstd = m.sb("var", [P, GT]), m.sb("rstd", [P, GT])
        tp, hp, ya, yo = ([m.ps(f"{n}{i}") for i in range(2)] for n in ("tp", "hp", "ya", "yo"))
        h_loaded, x_loaded, x_stored = m.sems("h_loaded", 2), m.sems("x_loaded", 2), m.sems("x_stored", 2)
        (head_steps, centred, squared, on_ready, tp_ready, tp_copied, ya_ready, ya_read, yo_ready, yo_read,
         merged_stats, x1_stats, out_stats, x1_ready, xn_ready, hid_ready, gelu_done, out_ready) = (m.sem(n) for n in (
             "head_steps", "centred", "squared", "on_ready", "tp_ready", "tp_copied", "ya_ready", "ya_read", "yo_ready", "yo_read",
             "merged_stats", "x1_stats", "out_stats", "x1_ready", "xn_ready", "hid_ready", "gelu_done", "out_ready"))
        ternary_ready = m.sem("ternary_ready")
        power = Power(m, C)
        hg = heads.rearrange("(b h) p (c w) -> b c p h w", b=B, c=GB)
        xg = x_in.rearrange("(g t p) e -> g p t e", p=P, t=GT)
        og = x_out.rearrange("(g t p) e -> g p t e", p=P, t=GT)
        NTP = HC + EC
        block = ctx.enter_context(nc.Block())

        @block.sync
        def _(sp):
            def load(g, i, r):
                sp.dma_start(os_[:, r].rearrange("p h t v -> p h (t v)"), at(hg[:, r], i)).then_inc(h_loaded[r], 16)
                sp.dma_start(xs[:, r], at(xg, g)).then_inc(x_loaded[r], 16)

            def body(g, i, r, left):
                sp.wait_ge(x1_ready, g + 1)
                if left >= 2:
                    load(g + 2, i + 1, r)
                sp.wait_ge(out_ready, g + 1)
                sp.dma_start(at(og, g), xo[:, r]).then_inc(x_stored[r], 16)

            for g in range(2):
                load(g, 0, g)
            turns(sp, G, 2, body)
            for r in range(2):
                sp.wait_ge(x_stored[r], 16 * (G // 2 + 1))

        @block.gpsimd
        def _(pool):
            def merged(k):
                power.serve(nc, pool, var[:], rstd[:], k)
                power.serve(nc, pool, var[:], rstd[:], k + 1)

            def body(g, i, r, left):
                if left:
                    merged(4 + 4 * g)
                if left >= 2:
                    power.serve(nc, pool, hv[:], hr[:], 4 + 4 * g + 2)
                power.serve(nc, pool, var[:], rstd[:], 4 + 4 * g + (3, 2, -1)[2 - left])

            power.serve(nc, pool, hv[:], hr[:], 0)
            merged(1)
            power.serve(nc, pool, hv[:], hr[:], 3)
            turns(pool, G, 2, body)

        @block.tensor
        def _(pe):
            pe.wait_ge(C["s_ffn"], 48)

            def merge(g, base):
                pe.wait_ge(on_ready, g + 1)
                for c in range(HC):
                    wait_pos(pe, tp_copied, base + c - 1)
                    for t in range(GT):
                        ins = nc.tensor.transpose(tp[c % 2][:, t * P:(t + 1) * P], on[:, t, c * P:(c + 1) * P], C["ident"][:])
                    ins.then_inc(tp_ready, 1)
                for t in range(GT):
                    pe.wait_ge(tp_copied, base + HC)
                    if t % 2 == 0:
                        wait_pos(pe, ya_read, g)
                    for c in range(HC):
                        ins = nc.tensor.matmul(ya[t // 2][:, t % 2 * E:(t % 2 + 1) * E], mt[:, c, t * P:(t + 1) * P],
                                               C["wo"][:, c], start=(c == 0), stop=(c == HC - 1))
                    ins.then_inc(ya_ready, 1)

            def turn_x(g, base):
                pe.wait_ge(xn_ready, g + 1)
                for c in range(EC):
                    pe.wait_ge(tp_copied, base + HC + c - 1)
                    for t in range(GT):
                        ins = nc.tensor.transpose(tp[c % 2][:, t * P:(t + 1) * P], xn[:, t, c * P:(c + 1) * P], C["ident"][:])
                    ins.then_inc(tp_ready, 1)

            def body(g, i, r, left):
                pe.wait_ge(tp_copied, (g + 1) * NTP)
                for n in range(FM):
                    pe.wait_ge(gelu_done, g * FM + n + 1)
                    for c in range(EC):
                        ins = nc.tensor.matmul(hp[n % 2][:], C["w1t"][:, c, n * P:(n + 1) * P], xt[:, c],
                                               start=(c == 0), stop=(c == EC - 1))
                    ins.then_inc(hid_ready, 1)
                if left:
                    merge(g + 1, (g + 1) * NTP)
                pe.wait_ge(gelu_done, (g + 1) * FM + 2)
                for t in range(GT):
                    if t % 2 == 0:
                        wait_pos(pe, yo_read, 2 * g - 1 + t // 2)
                    for n in range(FM):
                        ins = nc.tensor.matmul(yo[t // 2][:, t % 2 * E:(t % 2 + 1) * E], ht[:, n, t * P:(t + 1) * P],
                                               C["w2t"][:, n], start=(n == 0), stop=(n == FM - 1))
                    ins.then_inc(yo_ready, 1)
                if left:
                    turn_x(g + 1, (g + 1) * NTP)

            merge(0, 0)
            turn_x(0, 0)
            pe.wait_ge(ternary_ready, 10)
            turns(pe, G, 2, body)

        @block.scalar
        def _(act):
            act.sem_inc(gelu_done, 2)

            def square(g):
                act.wait_ge(centred, g + 1)
                act.activation(sq[:], xc[:], ACT.Square).then_inc(squared, 1)

            def merged(base):
                for c in range(HC):
                    act.wait_ge(tp_ready, base + c + 1)
                    act.activation(mt[:, c], tp[c % 2][:], ACT.Copy).then_inc(tp_copied, 1)

            def x_group(base):
                for c in range(EC):
                    act.wait_ge(tp_ready, base + HC + c + 1)
                    act.activation(xt[:, c], tp[c % 2][:], ACT.Copy).then_inc(tp_copied, 1)

            def body(g, i, r, left):
                for n in range(FM):
                    act.wait_ge(hid_ready, g * FM + n + 1)
                    act.activation(ht[:, n], hp[n % 2][:], ACT.Gelu, bias=C["b1"][:, n:n + 1]).then_inc(gelu_done, 1)
                if left:
                    merged((g + 1) * NTP)
                if left >= 2:
                    square(g + 2)
                if left:
                    x_group((g + 1) * NTP)

            square(0)
            merged(0)
            square(1)
            x_group(0)
            turns(act, G, 2, body)

        @block.vector
        def _(v):
            for r in range(2):
                v.sem_inc(x_stored[r], 16)
            hch, ach = Chain(v, head_steps, 4), Chain(v, merged_stats, 3 * GT - 1)
            bch, cch = Chain(v, x1_stats, 2 * GT), Chain(v, out_stats, 3 * GT)

            def head_centre(g, r, uses):
                hch.turn(g)
                v.wait_ge(h_loaded[r], 16 * uses)
                src = os_[:, r].rearrange("p h t v -> p (h t) v")
                shape = [P, H * GT, VD]
                hch.link(v.tensor_reduce(hm[:], src, AX.X, ALU.add))
                hch.link(v.tensor_scalar(hm[:], hm[:], 1.0 / VD, None, ALU.mult))
                v.tensor_tensor(xc[:], src, bcast(hm[:].unsqueeze(2), shape), ALU.subtract).then_inc(centred, 1)
                v.wait_ge(squared, g + 1)
                hch.link(v.tensor_reduce(hv[:], sq[:], AX.X, ALU.add))

            def head_var():
                power.request(v.tensor_scalar(hv[:], hv[:], 1.0 / VD, EPS, ALU.mult, ALU.add))

            def head_norm(k):
                power.receive(v, k)
                hch.link(v.tensor_scalar(hr[:], hr[:], 1.0 - LAM_INIT, None, ALU.mult))
                dst = on[:].rearrange("p t (h v) -> p h t v", h=H)
                hrv = hr[:].rearrange("p (h t) -> p h t", h=H)
                for t in range(GT):
                    ins = v.tensor_tensor(dst[:, :, t], xc[:].rearrange("p (h t) v -> p h t v", h=H)[:, :, t],
                                          bcast(hrv[:, :, t:t + 1], [P, H, VD]), ALU.mult)
                ins.then_inc(on_ready, 1)

            def merged(g, r, uses, k):
                ach.turn(g)
                bch.turn(g)
                v.wait_ge(ya_ready, (g + 1) * GT)
                y = lambda t: ya[t // 2][:, t % 2 * E:(t % 2 + 1) * E]
                mean_var(v, ach, C["go"], y, stats, mv, GT)
                power.ask(v, v.tensor_scalar(var[:], mv[:, :, 1], EPS, None, ALU.add), k)
                for t in range(GT):
                    ins = v.tensor_scalar(yn[:, t], y(t), mv[:, t, 0:1], rstd[:, t:t + 1], ALU.subtract, ALU.mult)
                    if t == GT - 1:
                        ins.then_inc(ya_read, 1)
                    else:
                        ach.mark(ins)
                v.wait_ge(ya_read, g + 1)
                v.wait_ge(x_loaded[r], 16 * uses)
                v.tensor_tensor(x1[:, r], xs[:, r], yn[:], ALU.add).then_inc(x1_ready, 1)
                v.wait_ge(x1_ready, g + 1)
                mean_var(v, bch, C["go"], lambda t: x1[:, r, t], stats, mv, GT)
                power.ask(v, v.tensor_scalar(var[:], mv[:, :, 1], EPS, None, ALU.add), k + 1)
                for t in range(GT):
                    ins = v.tensor_scalar(xn[:, t], x1[:, r, t], mv[:, t, 0:1], rstd[:, t:t + 1], ALU.subtract, ALU.mult)
                ins.then_inc(xn_ready, 1)

            def finish_stats(g):
                cch.turn(g)
                wait_pos(v, out_ready, g)
                for n in range(2):
                    v.wait_ge(yo_ready, g * GT + 2 * n + 2)
                    v.tensor_tensor(yb[:, 2 * n:2 * n + 2], yo[n][:].rearrange("p (t e) -> p t e", t=2),
                                    bcast(C["b2"][:].unsqueeze(1), [P, 2, E]), ALU.add).then_inc(yo_read, 1)
                v.wait_ge(yo_read, 2 * g + 2)
                mean_var(v, cch, C["go"], lambda t: yb[:, t], stats, mv, GT)
                power.request(v.tensor_scalar(var[:], mv[:, :, 1], EPS, None, ALU.add))

            def finish(g, i, r, k):
                power.receive(v, k)
                for t in range(GT):
                    cch.mark(v.tensor_scalar(yb[:, t], yb[:, t], mv[:, t, 0:1], rstd[:, t:t + 1], ALU.subtract, ALU.mult))
                v.wait_ge(x_stored[r], 16 * (i + 1))
                cch.wait()
                v.tensor_tensor(xo[:, r], x1[:, r], yb[:], ALU.add).then_inc(out_ready, 1)

            def body(g, i, r, left):
                if left >= 2:
                    head_centre(g + 2, r, i + 2)
                if left:
                    merged(g + 1, (r + 1) % 2, i + 1 + r, 4 + 4 * g)
                if left >= 2:
                    head_var()
                finish_stats(g)
                if left >= 2:
                    head_norm(4 + 4 * g + 2)
                finish(g, i, r, 4 + 4 * g + (3, 2, -1)[2 - left])

            def ternary(n):
                w = C[("w1t", "w2t")[n]][:].rearrange("p c n -> p (c n)")
                tern.link(v.tensor_scalar(neg, w, C["thr"][:, n, 1:2], None, ALU.is_lt))
                tern.link(v.tensor_scalar(wt, w, C["thr"][:, n, 0:1], None, ALU.is_gt))
                tern.link(v.tensor_tensor(wt, wt, neg, ALU.subtract))
                tern.link(v.tensor_tensor(wt, wt, w, ALU.subtract))
                tern.link(v.tensor_tensor(w, w, wt, ALU.add))

            neg, wt = (ht[:, n * FM // 2:(n + 1) * FM // 2].rearrange("p c n -> p (c n)") for n in range(2))
            tern = Chain(v, ternary_ready)
            head_centre(0, 0, 1)
            head_var()
            ternary(0)
            head_norm(0)
            head_centre(1, 1, 1)
            merged(0, 0, 1, 1)
            head_var()
            ternary(1)
            head_norm(3)
            turns(v, G, 2, body)


def convolve(nc, I, C, x_in, x_out):
    NT = 7
    VT = K - NT
    PRE_AT = 3
    GLU_AT = (2, 4, 6, 7)
    TILES = [(c, h) for c in range(EC) for h in range(GB)]
    NTL = len(TILES)
    with ExitStack() as ctx:
        m = Mem(nc, ctx, "cnv")
        xs, xn = m.sb("xs", [P, 2, SB, E]), m.sb("xn", [P, SB, E])
        xt = m.sb("xt", [P, EC, S])
        sg = m.sb("sg", [P, EC, S])
        gp = m.sb("gp", [P, 2, EC, S + 2 * PAD])
        acc = m.sb("acc", [P, EC, S])
        dg = m.sb("dg", [P, EC, NT, P])
        xo = m.sb("xo", [P, 2, SB, E])
        stats, mv, var, rstd = m.sb("stats", [P, SB, 6]), m.sb("mv", [P, SB, 2]), m.sb("var", [P, SB]), m.sb("rstd", [P, SB])
        tap, yo = [m.ps(f"tap{i}") for i in range(NTL)], [m.ps(f"yo{i}") for i in range(2)]
        ap, gpp = m.ps("a"), m.ps("g")
        tp = [ap, gpp]
        x_loaded, x_stored = m.sems("x_loaded", 2), m.sems("x_stored", 2)
        (edges, in_stats, tap_done, out_stats, xn_ready, tp_ready, tp_copied, a_ready, g_ready, sig_done, glu_done,
         taps_ready, taps_read, acc_ready, yo_ready, yo_read, out_ready) = (m.sem(n) for n in (
             "edges", "in_stats", "tap_done", "out_stats", "xn_ready", "tp_ready", "tp_copied", "a_ready", "g_ready", "sig_done",
             "glu_done", "taps_ready", "taps_read", "acc_ready", "yo_ready", "yo_read", "out_ready"))
        power = Power(m, C)
        xg = x_in.rearrange("(b t p) e -> b p t e", p=P, t=SB)
        og = x_out.rearrange("(b t p) e -> b p t e", p=P, t=SB)
        block = ctx.enter_context(nc.Block())

        @block.sync
        def _(sp):
            def body(b, i, r, left):
                sp.wait_ge(out_ready, b + 1)
                sp.dma_start(at(og, b), xo[:, r]).then_inc(x_stored[r], 16)
                if left >= 2:
                    sp.dma_start(xs[:, r], at(xg, b + 2)).then_inc(x_loaded[r], 16)

            for b in range(2):
                sp.dma_start(xs[:, b], at(xg, b)).then_inc(x_loaded[b], 16)
            turns(sp, B, 2, body)
            for r in range(2):
                sp.wait_ge(x_stored[r], 16 * (B // 2 + 1))

        @block.gpsimd
        def _(pool):
            def body(b, i, r, left):
                if left:
                    power.serve(nc, pool, var[:], rstd[:], 1 + 2 * b)
                power.serve(nc, pool, var[:], rstd[:], 1 + 2 * b + (1 if left else 0))

            power.serve(nc, pool, var[:], rstd[:], 0)
            turns(pool, B, 2, body)

        @block.tensor
        def _(pe):
            pe.wait_ge(C["s_conv"], 64)
            pe.wait_ge(edges, 2 + EC * NT)

            def gates(b):
                pe.wait_ge(xn_ready, b + 1)
                wait_pos(pe, glu_done, b * NTL)
                wait_pos(pe, sig_done, b * NTL)
                for n, (c, h) in enumerate(TILES):
                    wait_pos(pe, tp_copied, b * NTL + n - 1)
                    for t in range(GT):
                        ins = nc.tensor.transpose(tp[n % 2][:, t * P:(t + 1) * P], xn[:, h * GT + t, c * P:(c + 1) * P], C["ident"][:])
                    ins.then_inc(tp_ready, 1)
                pe.wait_ge(tp_copied, (b + 1) * NTL)
                for n, (c, h) in enumerate(TILES):
                    for dst, ready, read, col in ((gpp, g_ready, sig_done, E), (ap, a_ready, glu_done, 0)):
                        wait_pos(pe, read, b * NTL + n)
                        for k in range(EC):
                            ins = nc.tensor.matmul(dst[:], C["cw1"][:, k, col + c * P:col + (c + 1) * P],
                                                   xt[:, k, h * GN:(h + 1) * GN], start=(k == 0), stop=(k == EC - 1))
                        ins.then_inc(ready, 1)

            def taps(b, r):
                pe.wait_ge(glu_done, (b + 1) * NTL)
                for n, (c, h) in enumerate(TILES):
                    wait_pos(pe, taps_read, (b - 1) * NTL + n + 1)
                    for k in range(NT):
                        ins = nc.tensor.matmul(tap[n][:], dg[:, c, k], gp[:, r, c, h * GN + k:(h + 1) * GN + k],
                                               start=(k == 0), stop=(k == NT - 1))
                    ins.then_inc(taps_ready, 1)

            def body(b, i, r, left):
                if left:
                    gates(b + 1)
                pe.wait_ge(acc_ready, (b + 1) * NTL)
                for t in range(SB):
                    if t % 2 == 0:
                        wait_pos(pe, yo_read, b * (SB // 2) + t // 2 - 1)
                    for c in range(EC):
                        ins = nc.tensor.matmul(yo[t // 2 % 2][:, t % 2 * E:(t % 2 + 1) * E], acc[:, c, t * P:(t + 1) * P],
                                               C["cw2"][:, c], start=(c == 0), stop=(c == EC - 1))
                    ins.then_inc(yo_ready, 1)
                if left:
                    taps(b + 1, (r + 1) % 2)

            gates(0)
            taps(0, 0)
            turns(pe, B, 2, body)

        @block.scalar
        def _(act):
            def gates(b):
                for n, (c, h) in enumerate(TILES):
                    act.wait_ge(tp_ready, b * NTL + n + 1)
                    act.activation(xt[:, c, h * GN:(h + 1) * GN], tp[n % 2][:], ACT.Copy).then_inc(tp_copied, 1)
                wait_pos(act, glu_done, b * NTL)
                for n, (c, h) in enumerate(TILES):
                    act.wait_ge(g_ready, b * NTL + n + 1)
                    act.activation(sg[:, c, h * GN:(h + 1) * GN], gpp[:], ACT.Sigmoid, bias=C["cb1"][:, EC + c:EC + c + 1])\
                        .then_inc(sig_done, 1)

            gates(0)
            turns(act, B, 2, lambda b, i, r, left: gates(b + 1) if left else None)

        @block.vector
        def _(v):
            for r in range(2):
                v.sem_inc(x_stored[r], 16)
            v.wait_ge(C["s_conv"], 64)
            v.memset(gp[:, :, :, 0:PAD].rearrange("p s c n -> p (s c) n"), 0.0).then_inc(edges, 1)
            v.memset(gp[:, :, :, PAD + S:].rearrange("p s c n -> p (s c) n"), 0.0).then_inc(edges, 1)
            for c in range(EC):
                for k in range(NT):
                    v.tensor_scalar(dg[:, c, k], C["ident"][:], C["filt"][:, c, k:k + 1], None, ALU.mult).then_inc(edges, 1)
            v.wait_ge(edges, 2 + EC * NT)
            pch, tch, ych = Chain(v, in_stats, 2 * SB), Chain(v, tap_done, (K - NT - 2) * NTL), Chain(v, out_stats, 3 * SB)

            def pre_stats(b, r, uses):
                pch.turn(b)
                v.wait_ge(x_loaded[r], 16 * uses)
                mean_var(v, pch, C["go"], lambda t: xs[:, r, t], stats, mv, SB)
                power.request(v.tensor_scalar(var[:], mv[:, :, 1], EPS, None, ALU.add))

            def pre(b, r, k):
                power.receive(v, k)
                for t in range(SB):
                    ins = v.tensor_scalar(xn[:, t], xs[:, r, t], mv[:, t, 0:1], rstd[:, t:t + 1], ALU.subtract, ALU.mult)
                ins.then_inc(xn_ready, 1)

            def glu(b, r, n):
                c, h = TILES[n]
                wait_pos(v, acc_ready, (b - 1) * NTL)
                v.wait_ge(a_ready, b * NTL + n + 1)
                v.wait_ge(sig_done, b * NTL + n + 1)
                v.scalar_tensor_tensor(out=gp[:, r, c, PAD + h * GN:PAD + (h + 1) * GN], in0=ap[:], scalar=C["cb1"][:, c:c + 1],
                                       in1=sg[:, c, h * GN:(h + 1) * GN], op0=ALU.add, op1=ALU.mult).then_inc(glu_done, 1)

            def tap_round(b, r, c, k):
                for h in range(GB):
                    n = TILES.index((c, h))
                    a = acc[:, c, h * GN:(h + 1) * GN]
                    if k == NT:
                        v.wait_ge(taps_ready, b * NTL + n + 1)
                    elif k == NT + 1:
                        v.wait_ge(taps_read, b * NTL + n + 1)
                    else:
                        v.wait_ge(tap_done, tch.base + (c * (VT - 2) + k - NT - 2) * GB + h + 1)
                    ins = v.scalar_tensor_tensor(out=a, in0=gp[:, r, c, h * GN + k:(h + 1) * GN + k],
                                                 scalar=C["filt"][:, c, k:k + 1], in1=tap[n][:] if k == NT else a,
                                                 op0=ALU.mult, op1=ALU.add)
                    if k == NT:
                        ins.then_inc(taps_read, 1)
                    elif k == K - 1:
                        ins.then_inc(acc_ready, 1)
                    else:
                        tch.mark(ins)

            def finish(b, i, r, k):
                ych.turn(b)
                v.wait_ge(x_stored[r], 16 * (i + 1))
                for n in range(SB // 2):
                    v.wait_ge(yo_ready, b * SB + 2 * n + 2)
                    v.tensor_tensor(xo[:, r, 2 * n:2 * n + 2], yo[n % 2][:].rearrange("p (t e) -> p t e", t=2),
                                    bcast(C["cb2"][:].unsqueeze(1), [P, 2, E]), ALU.add).then_inc(yo_read, 1)
                v.wait_ge(yo_read, (b + 1) * (SB // 2))
                mean_var(v, ych, C["go"], lambda t: xo[:, r, t], stats, mv, SB)
                power.ask(v, v.tensor_scalar(var[:], mv[:, :, 1], EPS, None, ALU.add), k)
                for t in range(SB):
                    ych.mark(v.tensor_scalar(xo[:, r, t], xo[:, r, t], mv[:, t, 0:1], rstd[:, t:t + 1], ALU.subtract, ALU.mult))
                ych.wait()
                v.tensor_tensor(xo[:, r], xs[:, r], xo[:, r], ALU.add).then_inc(out_ready, 1)

            def body(b, i, r, left):
                tch.turn(b)
                v.wait_ge(glu_done, (b + 1) * NTL)
                for c in range(EC):
                    for k in range(VT):
                        tap_round(b, r, c, NT + k)
                        if c == 0 and k == PRE_AT and left:
                            pre_stats(b + 1, (r + 1) % 2, i + 1 + r)
                        if c == 0 and k == PRE_AT + 2 and left:
                            pre(b + 1, (r + 1) % 2, 1 + 2 * b)
                        if c == 1 and left:
                            for n in range(NTL):
                                if GLU_AT[n] == k:
                                    glu(b + 1, (r + 1) % 2, n)
                finish(b, i, r, 1 + 2 * b + (1 if left else 0))

            pre_stats(0, 0, 1)
            pre(0, 0, 0)
            for n in range(NTL):
                glu(0, 0, n)
            turns(v, B, 2, body)


def experts(nc, I, C, x_in, x_out):
    NEXT_AT = 9
    with ExitStack() as ctx:
        m = Mem(nc, ctx, "moe")
        xs, xn, xt = m.sb("xs", [P, 2, GT, E]), m.sb("xn", [P, GT, E]), m.sb("xt", [P, 2, EC, GN])
        si, hh = m.sb("si", [P, 2, GN]), m.sb("hh", [P, 2, GN])
        comb, combt = m.sb("comb", [P, 2, GT, NX]), m.sb("combt", [NE, 2, GN])
        ya, yb, xo = m.sb("ya", [P, GT, E]), m.sb("yb", [P, GT, E]), m.sb("xo", [P, 2, GT, E])
        stats, mv, var, rstd = m.sb("stats", [P, GT, 6]), m.sb("mv", [P, GT, 2]), m.sb("var", [P, GT]), m.sb("rstd", [P, GT])
        lg, ex, sc = m.sb("lg", [P, GT, NE]), m.sb("ex", [P, GT, NE]), m.sb("sc", [P, GT, NE])
        mx, sm = m.sb("mx", [P, GT]), m.sb("sm", [P, GT])
        pairs = m.sb("pairs", [P, GT * NG, 6])
        gs = m.sb("gs", [P, GT, NG])
        g1, g2, gr = m.sb("g1", [P, GT, NG, NG]), m.sb("g2", [P, GT, NG, NG]), m.sb("gr", [P, GT, NG])
        pen = m.sb("pen", [P, GT, NG])
        e1, e2, er = m.sb("e1", [P, GT, NE, NE]), m.sb("e2", [P, GT, NE, NE]), m.sb("er", [P, GT, NE])
        h1, h3, yp = ([m.ps(f"{n}{i}") for i in range(2)] for n in ("h1", "h3", "y"))
        tp = [m.ps(f"tp{i}") for i in range(2)]
        x_loaded, x_stored = m.sems("x_loaded", 2), m.sems("x_stored", 2)
        (in_stats, out_stats, xn_ready, tp_ready, xt_ready, lg_ready, lg_read, lg_shift, exp_done, route_steps, comb_ready,
         ct_ready, ct_copied, be_ready, be_read, h1_ready, h3_ready, silu_done, h_done, y_ready, y_read, out_ready, ones_set) = (m.sem(n) for n in (
             "in_stats", "out_stats", "xn_ready", "tp_ready", "xt_ready", "lg_ready", "lg_read", "lg_shift", "exp_done", "route_steps",
             "comb_ready", "ct_ready", "ct_copied", "be_ready", "be_read", "h1_ready", "h3_ready", "silu_done", "h_done",
             "y_ready", "y_read", "out_ready", "ones_set"))
        power = Power(m, C)
        xg = x_in.rearrange("(g t p) e -> g p t e", p=P, t=GT)
        og = x_out.rearrange("(g t p) e -> g p t e", p=P, t=GT)
        block = ctx.enter_context(nc.Block())

        @block.sync
        def _(sp):
            def body(g, i, r, left):
                sp.wait_ge(out_ready, g + 1)
                sp.dma_start(at(og, g), xo[:, r]).then_inc(x_stored[r], 16)
                if left >= 2:
                    sp.dma_start(xs[:, r], at(xg, g + 2)).then_inc(x_loaded[r], 16)

            for g in range(2):
                sp.dma_start(xs[:, g], at(xg, g)).then_inc(x_loaded[g], 16)
            turns(sp, G, 2, body)
            for r in range(2):
                sp.wait_ge(x_stored[r], 16 * (G // 2 + 1))

        @block.gpsimd
        def _(pool):
            pool.memset(comb[:, :, :, NE:NX].rearrange("p s t e -> p (s t) e"), 1.0).then_inc(ones_set, 1)

            def body(g, i, r, left):
                if left:
                    power.serve(nc, pool, var[:], rstd[:], 1 + 2 * g)
                power.serve(nc, pool, var[:], rstd[:], 1 + 2 * g + (1 if left else 0))

            power.serve(nc, pool, var[:], rstd[:], 0)
            turns(pool, G, 2, body)

        @block.tensor
        def _(pe):
            pe.wait_ge(C["s_moe"], C["n_moe"])

            def inputs(g, r):
                pe.wait_ge(xn_ready, g + 1)
                wait_pos(pe, be_read, 2 * g)
                for c in range(EC):
                    for t in range(GT):
                        ins = nc.tensor.transpose(tp[c][:, t * P:(t + 1) * P], xn[:, t, c * P:(c + 1) * P], C["ident"][:])
                    ins.then_inc(tp_ready, 1)
                pe.wait_ge(xt_ready, (g + 1) * EC)
                for t in range(GT):
                    for c in range(EC):
                        ins = nc.tensor.matmul(tp[0][:, t * NE:(t + 1) * NE], xt[:, r, c, t * P:(t + 1) * P], C["gw"][:, c],
                                               start=(c == 0), stop=(c == EC - 1))
                ins.then_inc(lg_ready, 1)

            def routing(g, r):
                pe.wait_ge(comb_ready, g + 1)
                for t in range(GT):
                    ins = nc.tensor.transpose(tp[0][0:NE, t * P:(t + 1) * P], comb[:, r, t, 0:NE], C["ident"][:])
                ins.then_inc(ct_ready, 1)

            def hidden(g, r, x):
                n = g * NX + x
                for w, dst, ready, read in ((C["xw1"], h1, h1_ready, silu_done), (C["xw3"], h3, h3_ready, h_done)):
                    wait_pos(pe, read, n - 1)
                    for c in range(EC):
                        ins = nc.tensor.matmul(dst[x % 2][:], w[:, c, x], xt[:, r, c], start=(c == 0), stop=(c == EC - 1))
                    ins.then_inc(ready, 1)

            def down(g, x):
                n = g * NX + x
                pe.wait_ge(h_done, n + 1)
                for t in range(GT):
                    if t % 2 == 0:
                        wait_pos(pe, y_read, GT * n - 2 + t)
                    nc.tensor.matmul(yp[t // 2][:, t % 2 * E:(t % 2 + 1) * E], hh[:, x % 2, t * P:(t + 1) * P],
                                     C["xw2"][:, x], start=True, stop=True).then_inc(y_ready, 1)

            def biases(g, r, n):
                pe.wait_ge(ct_copied, g + 1)
                if n:
                    pe.wait_ge(be_read, 2 * g + 1)
                for t in (2 * n, 2 * n + 1):
                    ins = nc.tensor.matmul(tp[1][:, t % 2 * E:(t % 2 + 1) * E], combt[:, r, t * P:(t + 1) * P], C["xb2"][:],
                                           start=True, stop=True)
                ins.then_inc(be_ready, 1)

            def body(g, i, r, left):
                pe.wait_ge(xt_ready, (g + 1) * EC)
                for x in range(NX):
                    hidden(g, r, x)
                    if x == 1:
                        routing(g, r)
                    if x in (3, 5):
                        biases(g, r, (x - 3) // 2)
                    if x:
                        down(g, x - 1)
                    if x == NEXT_AT and left:
                        inputs(g + 1, (r + 1) % 2)
                down(g, NX - 1)

            inputs(0, 0)
            turns(pe, G, 2, body)

        @block.scalar
        def _(act):
            def inputs(g, r):
                for c in range(EC):
                    act.wait_ge(tp_ready, g * EC + c + 1)
                    act.activation(xt[:, r, c], tp[c][:], ACT.Copy).then_inc(xt_ready, 1)

            def exps(g):
                act.wait_ge(lg_shift, g + 1)
                act.activation(ex[:], lg[:], ACT.Exp).then_inc(exp_done, 1)

            def body(g, i, r, left):
                for x in range(NX):
                    n = g * NX + x
                    act.wait_ge(h1_ready, n + 1)
                    wait_pos(act, h_done, n - 1)
                    act.activation(si[:, x % 2], h1[x % 2][:], ACT.Silu, bias=C["xb1"][:, x:x + 1]).then_inc(silu_done, 1)
                    if x == 1:
                        act.wait_ge(ct_ready, g + 1)
                        act.activation(combt[:, r], tp[0][0:NE, :], ACT.Copy).then_inc(ct_copied, 1)
                    if x == NEXT_AT and left:
                        inputs(g + 1, (r + 1) % 2)
                    if x == NEXT_AT + 2 and left:
                        exps(g + 1)

            inputs(0, 0)
            exps(0)
            turns(act, G, 2, body)

        @block.vector
        def _(v):
            v.wait_ge(ones_set, 1)
            for r in range(2):
                v.sem_inc(x_stored[r], 16)
            pch, ych, rc = Chain(v, in_stats, 2 * GT), Chain(v, out_stats, 3 * GT), Chain(v, route_steps, 22)

            def pre_stats(g, r, uses):
                pch.turn(g)
                v.wait_ge(x_loaded[r], 16 * uses)
                mean_var(v, pch, C["go"], lambda t: xs[:, r, t], stats, mv, GT)
                power.request(v.tensor_scalar(var[:], mv[:, :, 1], EPS, None, ALU.add))

            def pre(g, r, k):
                power.receive(v, k)
                for t in range(GT):
                    ins = v.tensor_scalar(xn[:, t], xs[:, r, t], mv[:, t, 0:1], rstd[:, t:t + 1], ALU.subtract, ALU.mult)
                ins.then_inc(xn_ready, 1)

            def shift(g):
                rc.turn(g)
                v.wait_ge(lg_ready, g + 1)
                logits = tp[0][:, 0:GT * NE].rearrange("p (t e) -> p t e", t=GT)
                rc.link(v.tensor_reduce(mx[:], logits, AX.X, ALU.max))
                v.tensor_tensor(lg[:], logits, bcast(mx[:].unsqueeze(2), [P, GT, NE]), ALU.subtract).then_inc(lg_shift, 1)

            def route(g, r):
                v.wait_ge(exp_done, g + 1)
                T3 = [P, GT, NE]
                rc.link(v.tensor_reduce(sm[:], ex[:], AX.X, ALU.add))
                rc.link(v.reciprocal(sm[:], sm[:]))
                rc.link(v.tensor_tensor(ex[:], ex[:], bcast(sm[:].unsqueeze(2), T3), ALU.mult))
                rc.link(v.tensor_tensor(sc[:], ex[:], C["gb"][:], ALU.add))
                s4 = sc[:].rearrange("p t (g e) -> p (t g) e", g=NG)
                rc.mark(v.tensor_tensor(pairs[:, :, 0:3], s4[:, :, 0:3], s4[:, :, 1:4], ALU.add))
                rc.mark(v.tensor_tensor(pairs[:, :, 3:5], s4[:, :, 0:2], s4[:, :, 2:4], ALU.add))
                rc.link(v.tensor_tensor(pairs[:, :, 5:6], s4[:, :, 0:1], s4[:, :, 3:4], ALU.add))
                rc.link(v.tensor_reduce(gs[:].rearrange("p t g -> p (t g)"), pairs[:], AX.X, ALU.max))

                def rank(val, n, one, two, out, tri):
                    shape = [P, GT, n, n]
                    other, own = bcast(val.unsqueeze(2), shape), bcast(val.unsqueeze(3), shape)
                    rc.mark(v.tensor_tensor(one[:], other, own, ALU.is_gt))
                    rc.link(v.tensor_tensor(two[:], other, own, ALU.is_equal))
                    rc.link(v.tensor_tensor(two[:], two[:], bcast(tri.unsqueeze(1), shape), ALU.mult))
                    rc.link(v.tensor_tensor(one[:], one[:], two[:], ALU.add))
                    rc.link(v.tensor_reduce(out[:], one[:], AX.X, ALU.add))

                rank(gs[:], NG, g1, g2, gr, C["tri_g"][:])
                rc.link(v.tensor_scalar(gr[:], gr[:], 1.5, None, ALU.is_lt))
                rc.link(v.tensor_scalar(pen[:], gr[:], 1.0, BIG, ALU.subtract, ALU.mult))
                s5 = sc[:].rearrange("p t (g e) -> p t g e", g=NG)
                rc.link(v.tensor_tensor(s5, s5, bcast(pen[:].unsqueeze(3), [P, GT, NG, EPG]), ALU.add))
                rank(sc[:], NE, e1, e2, er, C["tri_e"][:])
                v.scalar_tensor_tensor(out=comb[:, r, :, 0:NE], in0=er[:], scalar=1.5, in1=ex[:], op0=ALU.is_lt, op1=ALU.mult)\
                    .then_inc(comb_ready, 1)

            def gate(g, x):
                n = g * NX + x
                v.wait_ge(h3_ready, n + 1)
                v.wait_ge(silu_done, n + 1)
                wait_pos(v, y_ready, GT * (n - 1))
                v.scalar_tensor_tensor(out=hh[:, x % 2], in0=h3[x % 2][:], scalar=C["xb3"][:, x:x + 1], in1=si[:, x % 2],
                                       op0=ALU.add, op1=ALU.mult).then_inc(h_done, 1)

            def add(g, r, x):
                n = g * NX + x
                if x == 0:
                    wait_pos(v, out_ready, g)
                for t in range(GT):
                    if t % 2 == 0:
                        v.wait_ge(y_ready, GT * n + t + 2)
                    if x:
                        v.wait_ge(y_read, GT * (n - 1) + t + 1)
                    v.scalar_tensor_tensor(out=ya[:, t], in0=yp[t // 2][:, t % 2 * E:(t % 2 + 1) * E],
                                           scalar=comb[:, r, t, x:x + 1], in1=C["bs2"][:] if x == 0 else ya[:, t],
                                           op0=ALU.mult, op1=ALU.add).then_inc(y_read, 1)

            def finish(g, r, uses, k):
                ych.base, ych.n = g * ych.per, 2 * GT
                power.receive(v, k)
                for t in range(GT):
                    ych.mark(v.tensor_scalar(yb[:, t], ya[:, t], mv[:, t, 0:1], rstd[:, t:t + 1], ALU.subtract, ALU.mult))
                v.wait_ge(x_stored[r], 16 * uses)
                ych.wait()
                v.tensor_tensor(xo[:, r], xs[:, r], yb[:], ALU.add).then_inc(out_ready, 1)

            def body(g, i, r, left):
                v.wait_ge(comb_ready, g + 1)
                for x in range(NX):
                    gate(g, x)
                    if x:
                        add(g, r, x - 1)
                    if x in (4, 6):
                        n = (x - 4) // 2
                        v.wait_ge(be_ready, 2 * g + n + 1)
                        v.wait_ge(y_read, GT * (g * NX + x))
                        v.tensor_tensor(ya[:, 2 * n:2 * n + 2], ya[:, 2 * n:2 * n + 2],
                                        tp[1][:].rearrange("p (t e) -> p t e", t=2), ALU.add).then_inc(be_read, 1)
                        v.wait_ge(be_read, 2 * g + n + 1)
                    if x == 0 and not (isinstance(g, int) and g == 0):
                        finish(g - 1, (r - 1) % 2, i + r, 2 * g)
                    if x == 5 and left:
                        pre_stats(g + 1, (r + 1) % 2, i + 1 + r)
                    if x == 6 and left:
                        pre(g + 1, (r + 1) % 2, 1 + 2 * g)
                    if x == NEXT_AT + 1 and left:
                        shift(g + 1)
                    if x == NEXT_AT + 3 and left:
                        route(g + 1, (r + 1) % 2)
                add(g, r, NX - 1)
                v.wait_ge(y_read, GT * NX * (g + 1))
                ych.turn(g)
                mean_var(v, ych, C["go"], lambda t: ya[:, t], stats, mv, GT)
                power.request(v.tensor_scalar(var[:], mv[:, :, 1], EPS, None, ALU.add))

            pre_stats(0, 0, 1)
            pre(0, 0, 0)
            shift(0)
            route(0, 0)
            turns(v, G, 2, body)
            finish(G - 1, (G - 1) % 2, G // 2, 2 * G - 1)


def program(nc, I, out):
    with ExitStack() as ctx:
        m = Mem(nc, ctx, "c")
        C = {
            "wqk": m.sb("wqk", [P, MATS, EC, E]), "wv": m.sb("wv", [P, EC, H * VD]),
            "w1t": m.sb("w1t", [P, EC, FF]), "w2t": m.sb("w2t", [P, FM, E]),
            "wo": m.sb("wo", [P, H * VD // P, E]), "b1": m.sb("b1", [P, FM]), "b2": m.sb("b2", [P, E]),
            "cw1": m.sb("cw1", [P, EC, 2 * E]), "cw2": m.sb("cw2", [P, EC, E]), "cb1": m.sb("cb1", [P, 2 * EC]),
            "cb2": m.sb("cb2", [P, E]), "filt": m.sb("filt", [P, EC, K]), "neglam": m.sb("neglam", [P, B * H]),
            "ident": m.sb("ident", [P, P]), "fold": m.sb("fold", [P, 2 * VO]),
            "thr": m.sb("thr", [P, 2, 2]), "identb": m.sb("identb", [P, P], BF16), "mask": m.sb("mask", [P, P], BF16),
            "tri_g": m.sb("tri_g", [P, NG, NG]), "tri_e": m.sb("tri_e", [P, NE, NE]), "neghalf": m.sb("neghalf", [P, H * GT]),
            "s_qkv": m.sem("s_qkv"), "s_ffn": m.sem("s_ffn"), "s_conv": m.sem("s_conv"), "s_moe": m.sem("s_moe"), "go": m.sem("go"),
            "xw1": m.sb("xw1", [P, EC, NX, INTER]), "xw3": m.sb("xw3", [P, EC, NX, INTER]), "xw2": m.sb("xw2", [P, NX, E]),
            "xb1": m.sb("xb1", [P, NX]), "xb3": m.sb("xb3", [P, NX]), "xb2": m.sb("xb2", [NE, E]), "bs2": m.sb("bs2", [P, E]),
            "gw": m.sb("gw", [P, EC, NE]), "gb": m.sb("gb", [P, GT, NE]),
        }
        parts = nc.dram_tensor("parts", (3, MATS, B * E, S), BF16, kind="Internal").ap()
        values = nc.dram_tensor("values", (B * H, P, SB * VC), F32, kind="Internal").ap()
        heads = nc.dram_tensor("heads", (B * H, P, SB * VD), F32, kind="Internal").ap()
        prepare(nc, I, C)
        project(nc, I, C, I["x"], parts, values)
        attend(nc, I, C, parts, values, heads)
        x2 = nc.dram_tensor("x2", (B * S, E), F32, kind="Internal").ap()
        x3 = nc.dram_tensor("x3", (B * S, E), F32, kind="Internal").ap()
        merge_and_ffn(nc, I, C, heads, I["x"], x2)
        convolve(nc, I, C, x2, x3)
        experts(nc, I, C, x3, out)


def layouts(a):
    import numpy as np

    c = np.ascontiguousarray
    by = lambda v, n: c(v.reshape(n, P).T)
    fold = np.zeros((2, 2, VC, 2, VO), np.float32)
    for mp in range(2):
        for n in range(VC - 1):
            fold[:, mp, n, mp, n] = 1
            fold[:, mp, n, mp, VD - 1] = -1
        fold[:, mp, VC - 1, mp, VD] = 1
    return {
        "fold": fold.reshape(P, 2 * VO),
        "x": c(a["L0_attn_x"].reshape(B * S, E)),
        "wqk": np.stack([a["L0_attn_Wq1"], a["L0_attn_Wq2"], a["L0_attn_Wk1"], a["L0_attn_Wk2"]]),
        "Wv": a["L0_attn_Wv"], "Wo": a["L0_attn_Wo"],
        "lq1": a["L0_attn_lq1"], "lk1": a["L0_attn_lk1"], "lq2": a["L0_attn_lq2"], "lk2": a["L0_attn_lk2"],
        "w1t": c(a["L0_ffn_W1"].T), "b1": by(a["L0_ffn_b1"], FM), "w2t": c(a["L0_ffn_W2"].T), "b2": a["L0_ffn_b2"],
        "cw1": a["L1_attn_W1"], "cb1": by(a["L1_attn_b1"], 2 * EC), "cw2": a["L1_attn_W2"], "cb2": a["L1_attn_b2"],
        "cw": a["L1_attn_conv_shared_weight"],
        "gw": c(a["L1_ffn_gate_w"].T), "gb": a["L1_ffn_gate_b"],
        "We1": a["L1_ffn_We1"], "We2": a["L1_ffn_We2"], "We3": a["L1_ffn_We3"],
        "ws1": a["L1_ffn_ws1"], "ws2": a["L1_ffn_ws2"], "ws3": a["L1_ffn_ws3"],
        "xb1": np.concatenate([c(a["L1_ffn_be1"].T), by(a["L1_ffn_bs1"], NSH)], axis=1),
        "xb3": np.concatenate([c(a["L1_ffn_be3"].T), by(a["L1_ffn_bs3"], NSH)], axis=1),
        "be2": a["L1_ffn_be2"], "bs2": a["L1_ffn_bs2"],
    }


def kernel(**inputs):
    import numpy as np
    import concourse.bacc as bacc
    from concourse.bass_utils import run_bass_kernel_spmd

    nc = bacc.Bacc("TRN2", target_bir_lowering=False, num_devices=1)
    arrays, aps = {}, {}
    for name, a in layouts({k: np.asarray(v) for k, v in inputs.items()}).items():
        arrays[f"in_{name}"] = np.ascontiguousarray(a)
        aps[name] = nc.dram_tensor(f"in_{name}", a.shape, mybir.dt.from_np(a.dtype), kind="ExternalInput").ap()
    out = nc.dram_tensor("out_x", (B * S, E), F32, kind="ExternalOutput").ap()
    program(nc, aps, out)
    r = run_bass_kernel_spmd(nc, [arrays], core_ids=[0])
    return r.results[0]["out_x"].reshape(B, S, E)
```
